# Optimizing a Trainium2 kernel written in Bass

```python
import numpy as np
import jax
import jax.numpy as jnp

def _softmax(x, axis=-1):
    return jax.nn.softmax(x, axis=axis)

def _gelu(x):
    return jax.nn.gelu(x, approximate=True)

def _silu(x):
    return jax.nn.silu(x)

def _sigmoid(x):
    return jax.nn.sigmoid(x)

def _layernorm(x, axis=-1, eps=1e-05):
    m = jnp.mean(x, axis=axis, keepdims=True)
    v = jnp.var(x, axis=axis, keepdims=True)
    return (x - m) / jnp.sqrt(v + eps)

def _scatter_add(tgt, idx, src, axis=0):
    return tgt.at[idx].add(src)

def _segment_sum(src, seg, n):
    return jax.ops.segment_sum(src, seg, n)
kernel_name = 'mk_xattn_seq_d1_seqx_r4_48f312'

def setup_inputs(seed: int=0):
    np.random.seed(seed)
    _w = jnp.asarray

    def _rec_inputs():
        import jax
        import jax.numpy as jnp
        _rk = jax.random.key(seed)
        x = -0.0002928 + 1 * jax.random.normal(jax.random.fold_in(_rk, 1), (32, 256, 256), jnp.float32)
        _lenS = 256 - jax.random.randint(jax.random.fold_in(_rk, 7), (32,), 0, max(1, 256 // 4) + 1, jnp.int32)
        _lenS2 = 77 - jax.random.randint(jax.random.fold_in(_rk, 8), (32,), 0, max(1, 77 // 4) + 1, jnp.int32)
        _ctx_1024P = jax.random.normal(jax.random.fold_in(_rk, 11), (32, 16, 256), jnp.float32)
        _ctx_1024c = jax.random.dirichlet(jax.random.fold_in(_rk, 511), 0.3 * jnp.ones((16,), jnp.float32), (32, 77))
        _ctx_1024t = jnp.einsum('bsk,bkd->bsd', _ctx_1024c, _ctx_1024P)
        _ctx_1024t = _ctx_1024t * jax.lax.rsqrt(jnp.mean(jnp.square(_ctx_1024t)) + 1e-12) * 0.953939
        ctx_1024 = -1.39393e-06 + 0.999914 * (_ctx_1024t + 0.3 * jax.random.normal(jax.random.fold_in(_rk, 611), (32, 77, 256), jnp.float32))
        _validS = jnp.arange(256)[None, :] < _lenS[:, None]
        _validS2 = jnp.arange(77)[None, :] < _lenS2[:, None]
        _causal = jnp.tril(jnp.ones((256, 256), dtype=bool))
        mask_BxSxS2_bk0 = jnp.logical_not(jnp.broadcast_to(_validS2[:, None, :], (32, 256, 77)))
        return (x, ctx_1024, mask_BxSxS2_bk0)
    x, ctx_1024, mask_BxSxS2_bk0 = _rec_inputs()

    def _L0_xattn_setup():
        import jax, jax.numpy as jnp
        import numpy as np
        EPS = 1e-05

        def layer_norm(x, w, b):
            mu = jnp.mean(x, axis=-1, keepdims=True)
            var = jnp.var(x, axis=-1, keepdims=True)
            return (x - mu) * jax.lax.rsqrt(var + EPS) * w + b
        key = jax.random.key(seed)
        ks = jax.random.split(key, 12)
        B, N, M, C = (2, 512, 512, 256)
        H = 16
        hid = 4 * C
        s = lambda d: 1.0 / np.sqrt(d)
        return {'x': jax.random.normal(ks[0], (B, N, C), jnp.float32), 'context': jax.random.normal(ks[1], (B, M, C), jnp.float32), 'xa_mask': jax.random.bernoulli(ks[2], 0.1, (B, N, M)), 'qn_w': jnp.ones((C,), jnp.float32), 'qn_b': jnp.zeros((C,), jnp.float32), 'cn_w': jnp.ones((C,), jnp.float32), 'cn_b': jnp.zeros((C,), jnp.float32), 'n2_w': jnp.ones((C,), jnp.float32), 'n2_b': jnp.zeros((C,), jnp.float32), 'q_w': jax.random.normal(ks[3], (C, C), jnp.float32) * s(C), 'kv_w': jax.random.normal(ks[4], (C, 2 * C), jnp.float32) * s(C), 'proj_w': jax.random.normal(ks[5], (C, C), jnp.float32) * s(C), 'proj_b': jnp.zeros((C,), jnp.float32), 'fc1_w': jax.random.normal(ks[6], (C, hid), jnp.float32) * s(C), 'fc1_b': jnp.zeros((hid,), jnp.float32), 'fc2_w': jax.random.normal(ks[7], (hid, C), jnp.float32) * s(hid), 'fc2_b': jnp.zeros((C,), jnp.float32)}
    _L0_xattn_all = _L0_xattn_setup()
    _L0_xattn_in = {k: v for k, v in _L0_xattn_all.items() if k in ('qn_w', 'qn_b', 'cn_w', 'cn_b', 'n2_w', 'n2_b', 'q_w', 'kv_w', 'proj_w', 'proj_b', 'fc1_w', 'fc1_b', 'fc2_w', 'fc2_b')}
    del _L0_xattn_all
    return {'x': x, 'ctx_1024': ctx_1024, 'mask_BxSxS2_bk0': mask_BxSxS2_bk0, 'L0_xattn_qn_w': _L0_xattn_in['qn_w'], 'L0_xattn_qn_b': _L0_xattn_in['qn_b'], 'L0_xattn_cn_w': _L0_xattn_in['cn_w'], 'L0_xattn_cn_b': _L0_xattn_in['cn_b'], 'L0_xattn_n2_w': _L0_xattn_in['n2_w'], 'L0_xattn_n2_b': _L0_xattn_in['n2_b'], 'L0_xattn_q_w': _L0_xattn_in['q_w'], 'L0_xattn_kv_w': _L0_xattn_in['kv_w'], 'L0_xattn_proj_w': _L0_xattn_in['proj_w'], 'L0_xattn_proj_b': _L0_xattn_in['proj_b'], 'L0_xattn_fc1_w': _L0_xattn_in['fc1_w'], 'L0_xattn_fc1_b': _L0_xattn_in['fc1_b'], 'L0_xattn_fc2_w': _L0_xattn_in['fc2_w'], 'L0_xattn_fc2_b': _L0_xattn_in['fc2_b']}

def reference(x, ctx_1024, mask_BxSxS2_bk0, L0_xattn_qn_w, L0_xattn_qn_b, L0_xattn_cn_w, L0_xattn_cn_b, L0_xattn_n2_w, L0_xattn_n2_b, L0_xattn_q_w, L0_xattn_kv_w, L0_xattn_proj_w, L0_xattn_proj_b, L0_xattn_fc1_w, L0_xattn_fc1_b, L0_xattn_fc2_w, L0_xattn_fc2_b):
    import jax
    import jax.numpy as jnp

    def _L0_xattn_ref(x, context, xa_mask, qn_w, qn_b, cn_w, cn_b, n2_w, n2_b, q_w, kv_w, proj_w, proj_b, fc1_w, fc1_b, fc2_w, fc2_b):
        import jax, jax.numpy as jnp
        import numpy as np
        EPS = 1e-05

        def layer_norm(x, w, b):
            mu = jnp.mean(x, axis=-1, keepdims=True)
            var = jnp.var(x, axis=-1, keepdims=True)
            return (x - mu) * jax.lax.rsqrt(var + EPS) * w + b
        B, N, C = x.shape
        M = context.shape[1]
        H = 16
        D = C // H
        scale = D ** (-0.5)
        xq = layer_norm(x, qn_w, qn_b)
        ctx = layer_norm(context, cn_w, cn_b)
        q = (xq @ q_w).reshape(B, N, H, D)
        kv = (ctx @ kv_w).reshape(B, M, 2, H, D)
        k, v = (kv[:, :, 0], kv[:, :, 1])
        attn = jnp.einsum('bnhd,bmhd->bhnm', q, k) * scale
        neg = -jnp.finfo(attn.dtype).max
        attn = jnp.where(xa_mask[:, None, :, :], neg, attn)
        attn = jax.nn.softmax(attn, axis=-1)
        out = jnp.einsum('bhnm,bmhd->bnhd', attn, v).reshape(B, N, C)
        out = out @ proj_w + proj_b
        x = x + out
        h = layer_norm(x, n2_w, n2_b)
        h = jax.nn.gelu(h @ fc1_w + fc1_b, approximate=False) @ fc2_w + fc2_b
        return x + h
    x = _L0_xattn_ref(x, ctx_1024, mask_BxSxS2_bk0, L0_xattn_qn_w, L0_xattn_qn_b, L0_xattn_cn_w, L0_xattn_cn_b, L0_xattn_n2_w, L0_xattn_n2_b, L0_xattn_q_w, L0_xattn_kv_w, L0_xattn_proj_w, L0_xattn_proj_b, L0_xattn_fc1_w, L0_xattn_fc1_b, L0_xattn_fc2_w, L0_xattn_fc2_b)
    return x

_drawn_inputs = setup_inputs


def setup_inputs(seed=0):
    import zlib

    import numpy as np

    out = dict(_drawn_inputs(seed))
    spreads = {'L0_xattn_qn_w': (1.0, 0.2),
     'L0_xattn_qn_b': (0.0, 0.38),
     'L0_xattn_cn_w': (1.0, 0.2),
     'L0_xattn_cn_b': (0.0, 0.1),
     'L0_xattn_n2_w': (1.0, 0.2),
     'L0_xattn_n2_b': (0.0, 0.1),
     'L0_xattn_proj_b': (0.0, 0.1),
     'L0_xattn_fc1_b': (0.0, 0.1),
     'L0_xattn_fc2_b': (0.0, 0.1)}
    factors = {}
    for name, (base, spread) in spreads.items():
        noise = np.random.default_rng([zlib.crc32(name.encode()), seed]).standard_normal(out[name].shape)
        drawn = base * np.exp(spread * noise) if base else spread * noise
        out[name] = jnp.asarray(drawn.astype(out[name].dtype))
    for name, factor in factors.items():
        out[name] = (out[name] * factor).astype(out[name].dtype)
    return out
```

```python
import concourse.bass as bass
from concourse import mybir
from contextlib import ExitStack


def xattn_block(nc, x, ctx, mask, qn_w, qn_b, cn_w, cn_b, n2_w, n2_b, q_w, kv_w, proj_w, proj_b,
                fc1_w, fc1_b, fc2_w, fc2_b, out):
    F32 = mybir.dt.float32
    F32R = mybir.dt.float32r
    BF16 = mybir.dt.bfloat16
    ALU = mybir.AluOpType
    ACT = mybir.ActivationFunctionType
    X = mybir.AxisListType.X

    B, N, C = x.shape
    M = ctx.shape[1]
    HID = fc1_w.shape[1]
    H, D = 16, 16
    P = 128
    EPS = 1e-5
    SCALE = float(D) ** -0.5
    MASKED = -float(2 ** 127)
    NB = 2
    PAIRS = B // NB
    TT = NB * N // P
    KC = C // P
    HC = HID // P
    G = H * D // P
    HG = H // G
    UNITS = TT * G
    BG = NB * G
    MP = -(-M // D) * D
    NM = HG * MP // P
    HM = HG // 2 * M
    TN = TT * P

    es = ExitStack()
    with es:
        def sb(name, shape, dt=F32):
            return es.enter_context(nc.sbuf_tensor(name, shape, dt))

        def sem(name):
            return es.enter_context(nc.semaphore(name))

        qw_hi, qw_lo = sb("qw_hi", [P, KC, C], F32R), sb("qw_lo", [P, KC, C], F32R)
        kvw_hi, kvw_lo = sb("kvw_hi", [P, KC, 2 * C], F32R), sb("kvw_lo", [P, KC, 2 * C], F32R)
        pw_hi, pw_lo = sb("pw_hi", [P, KC, C], F32R), sb("pw_lo", [P, KC, C], F32R)
        w1_hi, w1_lo = sb("w1_hi", [P, KC, HID], F32R), sb("w1_lo", [P, KC, HID], F32R)
        w2_hi, w2_lo = sb("w2_hi", [P, HC, C], F32R), sb("w2_lo", [P, HC, C], F32R)
        vecs = sb("vecs", [P, 6, KC])
        fc1b = sb("fc1b", [P, HC])
        bias = sb("bias", [P, 2 * G + HC])
        bv = sb("bv", [M, C])
        projb = sb("projb", [P, C])
        fc2b = sb("fc2b", [P, C])
        ident = sb("ident", [P, P])
        ident_bf = sb("ident_bf", [P, P], BF16)
        head_of = sb("head_of", [P, HG])
        chunk_head = sb("chunk_head", [P, NM, HG])
        neg_half = sb("neg_half", [P, TT + NB])
        eps = sb("eps", [P, TT + NB])
        NP = 4
        stage = sb("stage", [P, 6144])
        probs = [stage[:, u * HG * MP:(u + 1) * HG * MP].rearrange("p (h m) -> p h m", m=MP)
                 for u in range(NP)]
        flat = [p.rearrange("p h m -> p (h m)") for p in probs]
        o1 = NP * HG * MP
        probsT = [stage[:, o1 + k * NM * N:o1 + (k + 1) * NM * N].rearrange("p (c n) -> p c n", n=N)
                  for k in range(2)]
        o2 = o1 + 2 * NM * N
        g_f = [stage[:, o2 + k * TN:o2 + (k + 1) * TN] for k in range(2)]
        assert o2 + 2 * TN == 6144
        raw_at = [0, KC * C, 3 * KC * C, 4 * KC * C, 4 * KC * C + KC * HID]
        raw_q = stage[:, raw_at[0]:raw_at[1]].rearrange("p (k n) -> p k n", k=KC)
        raw_kv = stage[:, raw_at[1]:raw_at[2]].rearrange("p (k n) -> p k n", k=KC)
        raw_p = stage[:, raw_at[2]:raw_at[3]].rearrange("p (k n) -> p k n", k=KC)
        raw_w1 = stage[:, raw_at[3]:raw_at[4]].rearrange("p (k n) -> p k n", k=KC)
        raw_w2 = stage[:, raw_at[4]:6144].rearrange("p (k n) -> p k n", k=HC)

        xin = [sb(f"xin{k}", [P, TT, C]) for k in range(2)]
        x1 = [sb(f"x1_{k}", [P, TT, C]) for k in range(2)]
        ctxin = sb("ctxin", [M, NB, C])
        xn = sb("xn", [P, TT, C])
        cn = sb("cn", [M, NB, C])
        stats = sb("stats", [P, TT + NB, 6])
        moms = sb("moms", [P, TT + NB, 2])
        rstd = sb("rstd", [P, TT + NB])
        stats2 = sb("stats2", [P, TT, 6])
        moms2 = sb("moms2", [P, TT, 2])
        rstd2 = sb("rstd2", [P, TT])
        hn = xn
        xT_hi, xT_lo = sb("xT_hi", [P, KC, TN], F32R), sb("xT_lo", [P, KC, TN], F32R)
        hT_hi, hT_lo = sb("hT_hi", [P, KC, TN], F32R), sb("hT_lo", [P, KC, TN], F32R)
        cT_hi, cT_lo = sb("cT_hi", [P, KC, NB * M], F32R), sb("cT_lo", [P, KC, NB * M], F32R)
        q_hi, q_lo = sb("q_hi", [P, G, TN], F32R), sb("q_lo", [P, G, TN], F32R)
        k_hi = sb("k_hi", [P, G, NB, M])
        k_lo = sb("k_lo", [P, G, NB, M])
        kd_hi = sb("kd_hi", [P, BG, HG * M], F32R)
        kd_lo = sb("kd_lo", [P, BG, HG * M], F32R)
        v_rows = sb("v_rows", [MP, NB * C])
        v_rep = sb("v_rep", [P, BG, NM, D])
        vd = sb("vd", [P, BG, NM, HG * D])
        mask_u8 = sb("mask_u8", [P, TT, M], mask.dtype)
        mask_b = [sb(f"mask_b{k}", [P, TT, M], BF16) for k in range(2)]
        rmax = [sb(f"rmax{k}", [P, HG]) for k in range(2)]
        carrier = sb("carrier", [P, 1])
        rsum = sb("rsum", [P, HG])
        rinv = [sb(f"rinv{k}", [P, HG, D]) for k in range(NP)]
        rinvT = sb("rinvT", [P, N])
        o_f = sb("o_f", [P, N])
        oT_hi, oT_lo = sb("oT_hi", [P, G, TN], F32R), sb("oT_lo", [P, G, TN], F32R)
        g_hi, g_lo = sb("g_hi", [P, HC, TN], F32R), sb("g_lo", [P, HC, TN], F32R)

        v_dram = nc.dram_tensor("v_dram", [2, NB * H, MP, D], F32, kind="Internal").ap()

        S = [es.enter_context(nc.psum_tensor(f"S{k}", [P, 2, 512], F32)) for k in range(2)]
        T = es.enter_context(nc.psum_tensor("T", [P, 512], F32))
        Q = es.enter_context(nc.psum_tensor("Q", [P, 512], F32))
        F = [es.enter_context(nc.psum_tensor(f"F{k}", [P, 512], F32)) for k in range(2)]

        consts = sem("consts")
        w_loaded = sem("w_loaded")
        vecs_loaded = sem("vecs_loaded")
        bias_mm = sem("bias_mm")
        w_hi_done = sem("w_hi_done")
        setup_done = sem("setup_done")
        x_loaded = sem("x_loaded")
        ctx_loaded = sem("ctx_loaded")
        mask_loaded = sem("mask_loaded")
        mask_ready = sem("mask_ready")
        stats_done = sem("stats_done")
        moms_done = sem("moms_done")
        rstd_step = sem("rstd_step")
        xn_done = sem("xn_done")
        cn_done = sem("cn_done")
        xb_done = sem("xb_done")
        cT_mm = sem("cT_mm")
        cT_hi_done = sem("cT_hi_done")
        cT_lo_done = sem("cT_lo_done")
        xT_mm = sem("xT_mm")
        xT_hi_done = sem("xT_hi_done")
        xT_lo_done = sem("xT_lo_done")
        k_mm = sem("k_mm")
        k_step = sem("k_step")
        kd_done = sem("kd_done")
        v_mm = sem("v_mm")
        v_rows_done = sem("v_rows_done")
        v_stored = sem("v_stored")
        v_gathered = sem("v_gathered")
        vd_done = sem("vd_done")
        q_mm = sem("q_mm")
        q_hi_done = sem("q_hi_done")
        q_lo_done = sem("q_lo_done")
        s_mm = sem("s_mm")
        max_done = sem("max_done")
        shifted = sem("shifted")
        exp_done = sem("exp_done")
        sum_done = sem("sum_done")
        rinv_done = sem("rinv_done")
        pT_mm = sem("pT_mm")
        pT_done = sem("pT_done")
        o_mm = sem("o_mm")
        rinvT_done = sem("rinvT_done")
        o_scaled = sem("o_scaled")
        o_hi_done = sem("o_hi_done")
        o_lo_done = sem("o_lo_done")
        proj_mm = sem("proj_mm")
        x1_done = sem("x1_done")
        stats2_done = sem("stats2_done")
        moms2_done = sem("moms2_done")
        rstd2_step = sem("rstd2_step")
        hn_done = sem("hn_done")
        x1b_done = sem("x1b_done")
        hT_mm = sem("hT_mm")
        hT_hi_done = sem("hT_hi_done")
        hT_lo_done = sem("hT_lo_done")
        f1_mm = sem("f1_mm")
        gelu_done = sem("gelu_done")
        g_hi_done = sem("g_hi_done")
        g_lo_done = sem("g_lo_done")
        f2_mm = sem("f2_mm")
        y_done = sem("y_done")
        y_stored = sem("y_stored")

        def least(n):
            return max(n, 0) if isinstance(n, int) else n

        def min_pair(j):
            return min(j, PAIRS) if isinstance(j, int) else j

        def pairs_of(eng, body):
            body(0, 0, False, True)
            body(1, 1, True, True)
            with eng.Fori(0, PAIRS // 2 - 2) as i:
                body(2 * i + 2, 0, True, True)
                body(2 * i + 3, 1, True, True)
            body(PAIRS - 2, 0, True, True)
            body(PAIRS - 1, 1, True, False)

        block = es.enter_context(nc.Block())

        @block.sync
        def _(sp):
            def load_pair(j, par):
                sp.wait_ge(consts, CONSTS)
                sp.wait_ge(x1_done, least(2 * (j - 1)))
                sp.dma_start(xin[par][:], x.rearrange("b (t p) c -> p (b t) c", p=P)[:, bass.ts(j, TT), :]).then_inc(x_loaded, 16)
                sp.wait_ge(consts, CONSTS)
                sp.wait_ge(cn_done, NB * j)
                sp.dma_start(ctxin[:], ctx.rearrange("b m c -> m b c")[:, bass.ts(j, NB), :]).then_inc(ctx_loaded, 16)
                sp.wait_ge(consts, CONSTS)
                sp.wait_ge(mask_ready, j)
                sp.dma_start(mask_u8[:], mask.rearrange("b (t p) m -> p (b t) m", p=P)[:, bass.ts(j, TT), :]).then_inc(mask_loaded, 16)

            def spread_v(j, par):
                sp.wait_ge(v_rows_done, j + 1)
                sp.dma_start(v_dram[par].rearrange("x m d -> m x d"), v_rows[:].rearrange("m (x d) -> m x d", d=D)).then_inc(v_stored, 16)
                sp.wait_ge(v_stored, 16 * (j + 1))
                sp.wait_ge(vd_done, BG * j)
                sp.dma_start(v_rep[:], v_dram[par].rearrange("(g h) m d -> g (h m) d", h=HG)
                             .rearrange("g (c p) d -> p g c d", p=P)).then_inc(v_gathered, 16)

            def store(j, par, half):
                sp.wait_ge(consts, CONSTS)
                sp.wait_ge(y_done, 2 * j + half + 1)
                dst = out.rearrange("b (t p) c -> p (b t) c", p=P)
                sp.dma_start(dst[:, bass.ds(j * TT + half * 2, 2), :], x1[par][:, 2 * half:2 * half + 2]).then_inc(y_stored, 16)

            for k, (dst, src) in enumerate(((raw_q, q_w), (raw_kv, kv_w), (raw_w1, fc1_w), (raw_p, proj_w), (raw_w2, fc2_w))):
                sp.dma_start(dst, src.rearrange("(k p) n -> p k n", p=P)).then_inc(w_loaded, 16)
            load_pair(0, 0)
            spread_v(0, 0)

            def body(j, par, mlp, prep):
                if prep:
                    load_pair(j + 1, 1 - par)
                    spread_v(j + 1, 1 - par)
                if mlp:
                    store(j - 1, 1 - par, 0)
                    store(j - 1, 1 - par, 1)
            pairs_of(sp, body)
            store(PAIRS - 1, 1, 0)
            store(PAIRS - 1, 1, 1)
            sp.wait_ge(y_stored, 32 * PAIRS)
            sp.wait_ge(v_stored, 16 * PAIRS)

        @block.gpsimd
        def _(pool):
            pool.memset(ident[:], 0.0).then_inc(consts, 1)
            pool.memset(head_of[:], 1.0).then_inc(consts, 1)
            pool.memset(chunk_head[:], 1.0).then_inc(consts, 1)
            pool.memset(neg_half[:], -0.5).then_inc(consts, 1)
            pool.memset(eps[:], EPS).then_inc(consts, 1)
            pool.memset(v_rows[:], 0.0).then_inc(consts, 1)
            pool.memset(moms[:], 1.0).then_inc(consts, 1)
            pool.wait_ge(consts, 7)
            pool.affine_select(out=ident[:], in_=ident[:], compare_op=ALU.not_equal, fill=1.0, base=0,
                               pattern=[[-1, P]], channel_multiplier=1).then_inc(consts, 1)
            pool.affine_select(out=head_of[:], in_=head_of[:], compare_op=ALU.is_ge, fill=0.0, base=0,
                               pattern=[[-D, HG]], channel_multiplier=1).then_inc(consts, 1)
            pool.affine_select(out=chunk_head[:], in_=chunk_head[:], compare_op=ALU.is_ge, fill=0.0, base=0,
                               pattern=[[P, NM], [-MP, HG]], channel_multiplier=1).then_inc(consts, 1)
            pool.wait_ge(consts, 10)
            pool.affine_select(out=head_of[:], in_=head_of[:], compare_op=ALU.is_ge, fill=0.0, base=D - 1,
                               pattern=[[D, HG]], channel_multiplier=-1).then_inc(consts, 1)
            pool.affine_select(out=chunk_head[:], in_=chunk_head[:], compare_op=ALU.is_ge, fill=0.0, base=MP - 1,
                               pattern=[[-P, NM], [MP, HG]], channel_multiplier=-1).then_inc(consts, 1)
            pool.wait_ge(consts, CONSTS)

            def rstd_x(j):
                pool.wait_ge(xn_done, TT * j)
                pool.wait_ge(cn_done, NB * j)
                pool.wait_ge(moms_done, (TT + NB) * (j + 1))
                pool.tensor_tensor(rstd[:], moms[:, :, 1], eps[:], ALU.add).then_inc(rstd_step, 1)
                pool.wait_ge(rstd_step, 2 * j + 1)
                pool.tensor_tensor(rstd[:], rstd[:], neg_half[:], ALU.pow).then_inc(rstd_step, 1)

            def rstd_h(j):
                pool.wait_ge(hn_done, TT * j)
                pool.wait_ge(moms2_done, TT * (j + 1))
                pool.tensor_tensor(rstd2[:], moms2[:, :, 1], eps[:, 0:TT], ALU.add).then_inc(rstd2_step, 1)
                pool.wait_ge(rstd2_step, 2 * j + 1)
                pool.tensor_tensor(rstd2[:], rstd2[:], neg_half[:, 0:TT], ALU.pow).then_inc(rstd2_step, 1)

            def add_proj_b(j, par):
                pool.wait_ge(xn_done, TT * (j + 1))
                pool.tensor_tensor(xin[par][:], xin[par][:], projb[:].unsqueeze(1).to_broadcast([P, TT, C]),
                                   ALU.add).then_inc(xb_done, 1)

            def add_fc2_b(j, par):
                pool.wait_ge(hn_done, TT * (j + 1))
                pool.tensor_tensor(x1[par][:], x1[par][:], fc2b[:].unsqueeze(1).to_broadcast([P, TT, C]),
                                   ALU.add).then_inc(x1b_done, 1)

            def spread_k(j, bg):
                b, g = divmod(bg, G)
                pool.wait_ge(k_step, (G + 2) * (j + 1))
                pool.wait_ge(s_mm, least(UNITS * (j - 1) + 2 * bg + 2))
                for part, src in ((kd_hi, k_hi), (kd_lo, k_lo)):
                    pool.tensor_tensor(part[:, bg].rearrange("p (h m) -> p h m", m=M),
                                       src[:, g, b].unsqueeze(1).to_broadcast([P, HG, M]),
                                       head_of[:].unsqueeze(2).to_broadcast([P, HG, M]), ALU.mult).then_inc(kd_done, 1)

            def spread_v(j, bg):
                pool.wait_ge(v_gathered, 16 * (j + 1))
                pool.wait_ge(o_mm, least(BG * (j - 1) + bg + 1))
                pool.tensor_tensor(vd[:, bg].rearrange("p c (h d) -> p c h d", d=D),
                                   v_rep[:, bg].unsqueeze(2).to_broadcast([P, NM, HG, D]),
                                   chunk_head[:].unsqueeze(3).to_broadcast([P, NM, HG, D]),
                                   ALU.mult).then_inc(vd_done, 1)

            def low_o(j, bg):
                b, g = divmod(bg, G)
                pool.wait_ge(o_scaled, BG * j + bg + 1)
                pool.wait_ge(o_hi_done, BG * j + bg + 1)
                pool.wait_ge(proj_mm, least(2 * (j - 1) + b + 1))
                cols = slice(b * N, (b + 1) * N)
                pool.tensor_tensor(oT_lo[:, g, cols], o_f[:], oT_hi[:, g, cols].bitcast(F32),
                                   ALU.subtract).then_inc(o_lo_done, 1)

            rstd_x(0)
            add_proj_b(0, 0)
            for bg in range(BG):
                spread_k(0, bg)
            for bg in range(BG):
                spread_v(0, bg)

            def body(j, par, mlp, prep):
                if prep:
                    rstd_x(j + 1)
                low_o(j, 0)
                if mlp:
                    add_fc2_b(j - 1, 1 - par)
                low_o(j, 1)
                if prep:
                    spread_v(j + 1, 0)
                    spread_k(j + 1, 0)
                    spread_k(j + 1, 1)
                    spread_k(j + 1, 2)
                low_o(j, 2)
                if prep:
                    add_proj_b(j + 1, 1 - par)
                low_o(j, 3)
                if prep:
                    spread_v(j + 1, 1)
                    spread_k(j + 1, 3)
                rstd_h(j)
                if prep:
                    spread_v(j + 1, 2)
                    spread_v(j + 1, 3)
            pairs_of(pool, body)
            add_fc2_b(PAIRS - 1, 1)

        @block.scalar
        def _(act):
            for k, v in enumerate((qn_w, qn_b, cn_w, cn_b, n2_w, n2_b)):
                act.dma_start(vecs[:, k], v.rearrange("(k p) -> p k", p=P), allow_slow_non_contiguous=True).then_inc(vecs_loaded, 16)
            act.dma_start(fc1b[:], fc1_b.rearrange("(k p) -> p k", p=P), allow_slow_non_contiguous=True).then_inc(vecs_loaded, 16)
            act.dma_start(projb[:], proj_b.unsqueeze(0).to_broadcast([P, C])).then_inc(vecs_loaded, 16)
            act.dma_start(fc2b[:], fc2_b.unsqueeze(0).to_broadcast([P, C])).then_inc(vecs_loaded, 16)
            act.wait_ge(vecs_loaded, 9 * 16)
            act.wait_ge(w_loaded, 5 * 16)
            for hi, raw, nw in ((qw_hi, raw_q, 0), (kvw_hi, raw_kv, 2), (w1_hi, raw_w1, 4)):
                for k in range(KC):
                    act.activation(hi[:, k], raw[:, k], ACT.Copy, scale=vecs[:, nw, k:k + 1]).then_inc(w_hi_done, 1)
            act.activation(pw_hi[:], raw_p, ACT.Copy).then_inc(w_hi_done, 1)
            act.activation(w2_hi[:], raw_w2, ACT.Copy).then_inc(w_hi_done, 1)

            def cT_high(j):
                act.wait_ge(cT_mm, j + 1)
                act.wait_ge(k_mm, j)
                act.wait_ge(v_mm, j)
                act.activation(cT_hi[:].rearrange("p k (b m) -> p k b m", m=M),
                               Q[:, 0:KC * NB * MP].rearrange("p (k b m) -> p k b m", k=KC, m=MP)[:, :, :, 0:M],
                               ACT.Copy).then_inc(cT_hi_done, 1)

            def xT_high(j, k):
                act.wait_ge(xT_mm, KC * j + k + 1)
                act.wait_ge(q_mm, G * j)
                act.activation(xT_hi[:, k], Q[:], ACT.Copy).then_inc(xT_hi_done, 1)

            def q_high(j, g):
                act.wait_ge(q_mm, G * j + g + 1)
                act.wait_ge(s_mm, least(UNITS * (j - 1) + 6 + 2 * g))
                act.activation(q_hi[:, g], Q[:], ACT.Identity, bias=bias[:, g:g + 1]).then_inc(q_hi_done, 1)

            def exp(j, u):
                act.wait_ge(shifted, UNITS * j + u + 1)
                act.activation(probs[u % NP][:, :, 0:M], probs[u % NP][:, :, 0:M], ACT.Exp, scale=SCALE).then_inc(exp_done, 1)

            def pT_copy(j, bg, s):
                n = 1 if s == 2 else 2
                act.wait_ge(pT_mm, 3 * (BG * j + bg) + s + 1)
                act.wait_ge(o_mm, least(BG * j + bg - 1))
                act.activation(probsT[bg % 2][:, 2 * s:2 * s + n], T[:, 0:n * N].rearrange("p (c n) -> p c n", n=N),
                               ACT.Copy).then_inc(pT_done, 1)

            def rinvT_copy(j, bg):
                act.wait_ge(o_mm, BG * j + bg + 1)
                act.wait_ge(o_scaled, BG * j + bg)
                act.activation(rinvT[:], Q[:, N:2 * N], ACT.Copy).then_inc(rinvT_done, 1)

            def hT_high(j, k):
                act.wait_ge(hT_mm, KC * j + k + 1)
                act.wait_ge(f1_mm, HC * j)
                act.activation(hT_hi[:, k], F[k][:], ACT.Copy).then_inc(hT_hi_done, 1)

            def gelu(j, k):
                act.wait_ge(f1_mm, HC * j + k + 1)
                act.wait_ge(g_lo_done, least(HC * j + max(k - 1, 0)))
                act.wait_ge(f2_mm, 2 * j)
                b1 = bias[:, 2 * G + k:2 * G + k + 1]
                act.activation(g_f[k % 2][:], F[k % 2][:], ACT.Gelu, bias=b1).then_inc(gelu_done, 1)
                act.activation(g_hi[:, k], F[k % 2][:], ACT.Gelu, bias=b1).then_inc(g_hi_done, 1)

            act.wait_ge(setup_done, SETUP)
            cT_high(0)
            xT_high(0, 0)
            xT_high(0, 1)
            q_high(0, 0)
            q_high(0, 1)

            def body(j, par, mlp, prep):
                exp(j, 0)
                if mlp:
                    hT_high(j - 1, 0)
                    hT_high(j - 1, 1)
                exp(j, 1)
                if mlp:
                    gelu(j - 1, 0)
                    gelu(j - 1, 1)
                pT_copy(j, 0, 0)
                if mlp:
                    gelu(j - 1, 2)
                pT_copy(j, 0, 1)
                if prep:
                    cT_high(j + 1)
                if mlp:
                    gelu(j - 1, 3)
                exp(j, 2)
                exp(j, 3)
                pT_copy(j, 0, 2)
                if mlp:
                    gelu(j - 1, 4)
                pT_copy(j, 1, 0)
                rinvT_copy(j, 0)
                exp(j, 4)
                pT_copy(j, 1, 1)
                exp(j, 5)
                if prep:
                    xT_high(j + 1, 0)
                pT_copy(j, 1, 2)
                if mlp:
                    gelu(j - 1, 5)
                pT_copy(j, 2, 0)
                rinvT_copy(j, 1)
                if mlp:
                    gelu(j - 1, 6)
                if prep:
                    xT_high(j + 1, 1)
                if mlp:
                    gelu(j - 1, 7)
                pT_copy(j, 2, 1)
                if prep:
                    q_high(j + 1, 0)
                exp(j, 6)
                exp(j, 7)
                pT_copy(j, 2, 2)
                pT_copy(j, 3, 0)
                pT_copy(j, 3, 1)
                rinvT_copy(j, 2)
                pT_copy(j, 3, 2)
                rinvT_copy(j, 3)
                if prep:
                    q_high(j + 1, 1)
            pairs_of(act, body)
            hT_high(PAIRS - 1, 0)
            hT_high(PAIRS - 1, 1)
            for k in range(HC):
                gelu(PAIRS - 1, k)

        @block.vector
        def _(dve):
            def low(dst, src, hi):
                return dve.tensor_tensor(dst, src, hi.bitcast(F32), ALU.subtract)

            def ln_stats(j, par):
                dve.wait_ge(rstd_step, 2 * j)
                dve.wait_ge(x_loaded, 16 * (j + 1))
                for t in range(TT):
                    dve.bn_stats(stats[:, t], xin[par][:, t]).then_inc(stats_done, 1)
                dve.wait_ge(ctx_loaded, 16 * (j + 1))
                for b in range(NB):
                    dve.bn_stats(stats[0:M, TT + b], ctxin[:, b]).then_inc(stats_done, 1)

            def ln_moments(j):
                dve.wait_ge(stats_done, (TT + NB) * (j + 1))
                dve.memset(carrier[:], 0.0)
                for t in range(TT):
                    dve.bn_aggr(moms[:, t], stats[:, t]).then_inc(moms_done, 1)
                for b in range(NB):
                    dve.bn_aggr(moms[0:M, TT + b], stats[0:M, TT + b]).then_inc(moms_done, 1)

            def normalise_ctx(j):
                dve.wait_ge(rstd_step, 2 * (j + 1))
                dve.wait_ge(cT_mm, j)
                for b in range(NB):
                    dve.tensor_scalar(cn[:, b], ctxin[:, b], moms[0:M, TT + b, 0:1], rstd[0:M, TT + b:TT + b + 1],
                                      ALU.subtract, ALU.mult).then_inc(cn_done, 1)

            def normalise_x(j, par):
                dve.wait_ge(rstd_step, 2 * (j + 1))
                dve.wait_ge(hT_mm, least(KC * (j - 1)))
                for t in range(TT):
                    dve.tensor_scalar(xn[:, t], xin[par][:, t], moms[:, t, 0:1], rstd[:, t:t + 1],
                                      ALU.subtract, ALU.mult).then_inc(xn_done, 1)

            def mask_bias(j, par):
                dve.wait_ge(mask_loaded, 16 * (j + 1))
                dve.wait_ge(s_mm, least(UNITS * (j - 1)))
                dve.tensor_scalar(mask_b[par][:], mask_u8[:], MASKED, None, ALU.mult).then_inc(mask_ready, 1)

            def cT_low(j):
                dve.wait_ge(cT_hi_done, j + 1)
                low(cT_lo[:].rearrange("p k (b m) -> p k b m", m=M),
                    Q[:, 0:KC * NB * MP].rearrange("p (k b m) -> p k b m", k=KC, m=MP)[:, :, :, 0:M],
                    cT_hi[:].rearrange("p k (b m) -> p k b m", m=M)).then_inc(cT_lo_done, 1)

            def xT_low(j, k):
                dve.wait_ge(xT_hi_done, KC * j + k + 1)
                low(xT_lo[:, k], Q[:], xT_hi[:, k]).then_inc(xT_lo_done, 1)

            def k_evacuate(j):
                dve.wait_ge(k_mm, j + 1)
                dve.wait_ge(kd_done, 2 * BG * j)
                for g in range(G):
                    dve.tensor_scalar(k_lo[:, g].rearrange("p b m -> p (b m)"), Q[:, g * NB * M:(g + 1) * NB * M],
                                      bias[:, G + g:G + g + 1], None, ALU.add).then_inc(k_step, 1)

            def k_split(j):
                dve.wait_ge(k_step, (G + 2) * j + G)
                dve.tensor_copy(k_hi[:].bitcast(F32R), k_lo[:]).then_inc(k_step, 1)
                dve.wait_ge(k_step, (G + 2) * j + G + 1)
                dve.tensor_tensor(k_lo[:], k_lo[:], k_hi[:], ALU.subtract).then_inc(k_step, 1)

            def v_evacuate(j):
                dve.wait_ge(v_mm, j + 1)
                dve.wait_ge(v_stored, 16 * j)
                dve.tensor_tensor(v_rows[0:M].rearrange("p (b c) -> p b c", c=C), Q[0:M, :].rearrange("p (b c) -> p b c", c=C),
                                  bv[:].unsqueeze(1).to_broadcast([M, NB, C]), ALU.add).then_inc(v_rows_done, 1)

            def q_low(j, g):
                dve.wait_ge(q_hi_done, G * j + g + 1)
                dve.scalar_tensor_tensor(out=q_lo[:, g], in0=Q[:], scalar=bias[:, g:g + 1],
                                         in1=q_hi[:, g].bitcast(F32), op0=ALU.add, op1=ALU.subtract).then_inc(q_lo_done, 1)

            def unit_views(u):
                return (S[u % 2][:, :, 0:HM].rearrange("p a (h m) -> p a h m", m=M),
                        rmax[u % 2][:].rearrange("p (a h) -> p a h", a=2))

            def row_max(j, u):
                sc, mx = unit_views(u)
                dve.wait_ge(s_mm, UNITS * j + u + 1)
                dve.wait_ge(shifted, least(UNITS * j + u - 1))
                dve.tensor_reduce(mx, sc, X, ALU.max).then_inc(max_done, 1)

            def shift(j, u):
                sc, mx = unit_views(u)
                dve.wait_ge(max_done, UNITS * j + u + 1)
                dve.wait_ge(pT_mm, least(3 * (BG * j + (u - NP) // 2 + 1)))
                dve.tensor_tensor(probs[u % NP][:, :, 0:M].rearrange("p (a h) m -> p a h m", a=2), sc,
                                  mx.unsqueeze(3).to_broadcast([P, 2, HG // 2, M]), ALU.subtract).then_inc(shifted, 1)

            def row_sum(j, u):
                dve.wait_ge(exp_done, UNITS * j + u + 1)
                dve.wait_ge(rinv_done, UNITS * j + u)
                dve.tensor_reduce(rsum[:], probs[u % NP][:, :, 0:M], X, ALU.add).then_inc(sum_done, 1)
                dve.wait_ge(sum_done, 2 * (UNITS * j + u) + 1)
                dve.wait_ge(o_mm, least(BG * j + (u - NP) // 2 + 1))
                dve.reciprocal(rsum[:], rsum[:]).then_inc(sum_done, 1)
                dve.wait_ge(sum_done, 2 * (UNITS * j + u + 1))
                dve.tensor_copy(rinv[u % NP][:], rsum[:].unsqueeze(2).to_broadcast([P, HG, D])).then_inc(rinv_done, 1)

            def o_scale(j, bg):
                dve.wait_ge(rinvT_done, BG * j + bg + 1)
                b, g = divmod(bg, G)
                dve.wait_ge(proj_mm, least(2 * (j - 1) + b + 1))
                dve.tensor_tensor(oT_hi[:, g, b * N:(b + 1) * N], Q[:, 0:N], rinvT[:], ALU.mult).then_inc(o_hi_done, 1)
                dve.wait_ge(o_lo_done, BG * j + bg)
                dve.tensor_tensor(o_f[:], Q[:, 0:N], rinvT[:], ALU.mult).then_inc(o_scaled, 1)

            def add_x(j, par, half):
                dve.wait_ge(proj_mm, 2 * j + half + 1)
                dve.wait_ge(xb_done, j + 1)
                dve.wait_ge(y_stored, least(32 * (j - 1)))
                dve.tensor_tensor(x1[par][:, 2 * half:2 * half + 2], Q[:].rearrange("p (t c) -> p t c", c=C),
                                  xin[par][:, 2 * half:2 * half + 2], ALU.add).then_inc(x1_done, 1)

            def h_stats(j, par, half):
                dve.wait_ge(x1_done, 2 * j + half + 1)
                dve.wait_ge(rstd2_step, 2 * j)
                for t in (2 * half, 2 * half + 1):
                    dve.bn_stats(stats2[:, t], x1[par][:, t]).then_inc(stats2_done, 1)

            def h_moments(j):
                dve.wait_ge(stats2_done, TT * (j + 1))
                dve.memset(carrier[:], 0.0)
                for t in range(TT):
                    dve.bn_aggr(moms2[:, t], stats2[:, t]).then_inc(moms2_done, 1)

            def h_normalise(j, par):
                dve.wait_ge(rstd2_step, 2 * (j + 1))
                dve.wait_ge(xT_mm, KC * min_pair(j + 2))
                for t in range(TT):
                    dve.tensor_scalar(hn[:, t], x1[par][:, t], moms2[:, t, 0:1], rstd2[:, t:t + 1],
                                      ALU.subtract, ALU.mult).then_inc(hn_done, 1)

            def hT_low(j, k):
                dve.wait_ge(hT_hi_done, KC * j + k + 1)
                low(hT_lo[:, k], F[k][:], hT_hi[:, k]).then_inc(hT_lo_done, 1)

            def g_low(j, k):
                dve.wait_ge(gelu_done, HC * j + k + 1)
                dve.wait_ge(g_hi_done, HC * j + k + 1)
                low(g_lo[:, k], g_f[k % 2][:], g_hi[:, k]).then_inc(g_lo_done, 1)

            def add_x1(j, par, half):
                dve.wait_ge(f2_mm, 2 * j + half + 1)
                dve.wait_ge(x1b_done, j + 1)
                dve.tensor_tensor(x1[par][:, 2 * half:2 * half + 2], F[half][:].rearrange("p (t c) -> p t c", c=C),
                                  x1[par][:, 2 * half:2 * half + 2], ALU.add).then_inc(y_done, 1)

            dve.wait_ge(consts, CONSTS)
            dve.tensor_copy(ident_bf[:], ident[:]).then_inc(setup_done, 1)
            dve.wait_ge(bias_mm, 2)
            dve.tensor_copy(bias[:, 0:2 * G], F[0][:, 0:2 * G]).then_inc(setup_done, 1)
            dve.tensor_tensor(bias[:, 2 * G:], F[0][:, 2 * G:2 * G + HC], fc1b[:], ALU.add).then_inc(setup_done, 1)
            dve.tensor_copy(bv[:], F[1][0:M, 0:C]).then_inc(setup_done, 1)
            done = 0
            for hi, lo, raw, nw in ((qw_hi, qw_lo, raw_q, 0), (kvw_hi, kvw_lo, raw_kv, 2), (w1_hi, w1_lo, raw_w1, 4)):
                for k in range(KC):
                    done += 1
                    dve.wait_ge(w_hi_done, done)
                    dve.scalar_tensor_tensor(out=lo[:, k], in0=raw[:, k], scalar=vecs[:, nw, k:k + 1],
                                             in1=hi[:, k].bitcast(F32), op0=ALU.mult, op1=ALU.subtract).then_inc(setup_done, 1)
            for hi, lo, raw in ((pw_hi, pw_lo, raw_p), (w2_hi, w2_lo, raw_w2)):
                done += 1
                dve.wait_ge(w_hi_done, done)
                low(lo[:], raw, hi[:]).then_inc(setup_done, 1)
            dve.wait_ge(setup_done, SETUP - NP)
            for u in range(NP):
                dve.memset(probs[u], 0.0).then_inc(setup_done, 1)
            dve.wait_ge(setup_done, SETUP)

            ln_stats(0, 0)
            mask_bias(0, 0)
            ln_moments(0)
            normalise_ctx(0)
            normalise_x(0, 0)
            cT_low(0)
            xT_low(0, 0)
            k_evacuate(0)
            k_split(0)
            xT_low(0, 1)
            v_evacuate(0)
            q_low(0, 0)
            q_low(0, 1)

            def body(j, par, mlp, prep):
                row_max(j, 0)
                if mlp:
                    h_normalise(j - 1, 1 - par)
                shift(j, 0)
                row_max(j, 1)
                shift(j, 1)
                if mlp:
                    hT_low(j - 1, 0)
                    hT_low(j - 1, 1)
                if prep:
                    ln_stats(j + 1, 1 - par)
                row_max(j, 2)
                if prep:
                    ln_moments(j + 1)
                row_max(j, 3)
                if mlp:
                    g_low(j - 1, 0)
                shift(j, 2)
                if prep:
                    normalise_ctx(j + 1)
                shift(j, 3)
                if mlp:
                    g_low(j - 1, 1)
                if prep:
                    cT_low(j + 1)
                row_sum(j, 0)
                if prep:
                    k_evacuate(j + 1)
                row_sum(j, 1)
                row_max(j, 4)
                if prep:
                    v_evacuate(j + 1)
                if mlp:
                    g_low(j - 1, 2)
                shift(j, 4)
                row_max(j, 5)
                if prep:
                    normalise_x(j + 1, 1 - par)
                shift(j, 5)
                o_scale(j, 0)
                row_sum(j, 2)
                row_sum(j, 3)
                if prep:
                    xT_low(j + 1, 0)
                if mlp:
                    g_low(j - 1, 3)
                    g_low(j - 1, 4)
                if prep:
                    k_split(j + 1)
                row_max(j, 6)
                o_scale(j, 1)
                if mlp:
                    g_low(j - 1, 5)
                    g_low(j - 1, 6)
                if prep:
                    xT_low(j + 1, 1)
                shift(j, 6)
                if mlp:
                    g_low(j - 1, 7)
                row_max(j, 7)
                shift(j, 7)
                if prep:
                    q_low(j + 1, 0)
                row_sum(j, 4)
                if prep:
                    mask_bias(j + 1, 1 - par)
                row_sum(j, 5)
                add_x(j, par, 0)
                row_sum(j, 6)
                row_sum(j, 7)
                o_scale(j, 2)
                o_scale(j, 3)
                h_stats(j, par, 0)
                if mlp:
                    add_x1(j - 1, 1 - par, 0)
                add_x(j, par, 1)
                h_stats(j, par, 1)
                h_moments(j)
                if mlp:
                    add_x1(j - 1, 1 - par, 1)
                if prep:
                    q_low(j + 1, 1)
            pairs_of(dve, body)
            h_normalise(PAIRS - 1, 1)
            hT_low(PAIRS - 1, 0)
            hT_low(PAIRS - 1, 1)
            for k in range(HC):
                g_low(PAIRS - 1, k)
            add_x1(PAIRS - 1, 1, 0)
            add_x1(PAIRS - 1, 1, 1)

        @block.tensor
        def _(pe):
            def product(dst, terms, inc=None):
                n = 0
                for (a_hi, a_lo), (b_hi, b_lo) in terms:
                    for a, b in ((a_hi, b_hi), (a_hi, b_lo), (a_lo, b_hi)):
                        last = pe.matmul(dst, a, b, start=(n == 0), stop=(n == 3 * len(terms) - 1))
                        n += 1
                return last

            def cT(j):
                pe.wait_ge(cn_done, NB * (j + 1))
                for k in range(KC):
                    for b in range(NB):
                        at = (k * NB + b) * MP
                        last = pe.transpose(Q[:, at:at + M], cn[:, b, k * P:(k + 1) * P], ident[0:M, 0:M])
                last.then_inc(cT_mm, 1)

            def xT(j, k):
                pe.wait_ge(xn_done, TT * (j + 1))
                for t in range(TT):
                    last = pe.transpose(Q[:, t * P:(t + 1) * P], xn[:, t, k * P:(k + 1) * P], ident[:])
                last.then_inc(xT_mm, 1)

            def k_proj(j):
                pe.wait_ge(cT_lo_done, j + 1)
                for g in range(G):
                    cols = slice(g * P, (g + 1) * P)
                    last = product(Q[:, g * NB * M:(g + 1) * NB * M],
                                   [((kvw_hi[:, k, cols], kvw_lo[:, k, cols]), (cT_hi[:, k], cT_lo[:, k])) for k in range(KC)])
                last.then_inc(k_mm, 1)

            def v_proj(j):
                for b in range(NB):
                    rows = slice(b * M, (b + 1) * M)
                    last = product(Q[0:M, b * C:(b + 1) * C],
                                   [((cT_hi[:, k, rows], cT_lo[:, k, rows]), (kvw_hi[:, k, C:], kvw_lo[:, k, C:])) for k in range(KC)])
                last.then_inc(v_mm, 1)

            def q_proj(j, g):
                pe.wait_ge(xT_lo_done, KC * (j + 1))
                cols = slice(g * P, (g + 1) * P)
                product(Q[:], [((qw_hi[:, k, cols], qw_lo[:, k, cols]), (xT_hi[:, k], xT_lo[:, k]))
                               for k in range(KC)]).then_inc(q_mm, 1)

            def scores(j, par, u):
                bg, t = divmod(u, 2)
                b, g = divmod(bg, G)
                tok = slice((2 * b + t) * P, (2 * b + t + 1) * P)
                pe.wait_ge(q_lo_done, G * j + g + 1)
                pe.wait_ge(kd_done, 2 * (BG * j + bg + 1))
                pe.wait_ge(mask_ready, j + 1)
                pe.wait_ge(shifted, least(UNITS * j + u - 1))
                for a in range(2):
                    dst = S[u % 2][:, a, 0:HM]
                    cols = slice(a * HM, (a + 1) * HM)
                    pe.matmul(dst.rearrange("p (h m) -> p h m", m=M), ident_bf[:],
                              mask_b[par][:, 2 * b + t].unsqueeze(1).to_broadcast([P, HG // 2, M]), start=True, stop=False)
                    pe.matmul(dst, q_hi[:, g, tok], kd_hi[:, bg, cols], start=False, stop=False)
                    pe.matmul(dst, q_hi[:, g, tok], kd_lo[:, bg, cols], start=False, stop=False)
                    last = pe.matmul(dst, q_lo[:, g, tok], kd_hi[:, bg, cols], start=False, stop=True)
                last.then_inc(s_mm, 1)

            def pT(j, bg, s):
                pe.wait_ge(exp_done, UNITS * j + 2 * bg + 2)
                pe.wait_ge(pT_done, 3 * (BG * j + bg) + s)
                for c in range(2 * s, min(2 * s + 2, NM)):
                    for t in range(2):
                        at = (c % 2) * N + t * P
                        last = pe.transpose(T[:, at:at + P], flat[(2 * bg + t) % NP][:, c * P:(c + 1) * P], ident[:])
                last.then_inc(pT_mm, 1)

            def attend(j, bg):
                pe.wait_ge(rinv_done, UNITS * j + 2 * bg + 2)
                for t in range(2):
                    pe.transpose(Q[:, N + t * P:N + (t + 1) * P],
                                 rinv[(2 * bg + t) % NP][:].rearrange("p h d -> p (h d)"), ident[:])
                pe.wait_ge(vd_done, BG * j + bg + 1)
                pe.wait_ge(pT_done, 3 * (BG * j + bg) + 3)
                for c in range(NM):
                    last = pe.matmul(Q[:, 0:N], vd[:, bg, c], probsT[bg % 2][:, c], start=(c == 0), stop=(c == NM - 1))
                last.then_inc(o_mm, 1)

            def project(j, half):
                pe.wait_ge(o_lo_done, BG * j + 2 * half + 2)
                for t in (2 * half, 2 * half + 1):
                    tok = slice(t * P, (t + 1) * P)
                    last = product(Q[:, (t % 2) * C:(t % 2 + 1) * C],
                                   [((oT_hi[:, g, tok], oT_lo[:, g, tok]), (pw_hi[:, g], pw_lo[:, g])) for g in range(G)])
                last.then_inc(proj_mm, 1)

            def hT(j, k):
                pe.wait_ge(hn_done, TT * (j + 1))
                pe.wait_ge(y_done, 2 * j)
                for t in range(TT):
                    last = pe.transpose(F[k][:, t * P:(t + 1) * P], hn[:, t, k * P:(k + 1) * P], ident[:])
                last.then_inc(hT_mm, 1)

            def fc1(j, k):
                pe.wait_ge(hT_lo_done, KC * (j + 1))
                if k >= 2:
                    pe.wait_ge(g_hi_done, least(HC * j + k - 1))
                cols = slice(k * P, (k + 1) * P)
                product(F[k % 2][:], [((w1_hi[:, c, cols], w1_lo[:, c, cols]), (hT_hi[:, c], hT_lo[:, c]))
                                      for c in range(KC)]).then_inc(f1_mm, 1)

            def fc2(j, t):
                pe.wait_ge(g_hi_done, HC * j + 7 + t // 2)
                pe.wait_ge(g_lo_done, HC * (j + 1))
                tok = slice(t * P, (t + 1) * P)
                last = product(F[t // 2][:, (t % 2) * C:(t % 2 + 1) * C],
                               [((g_hi[:, k, tok], g_lo[:, k, tok]), (w2_hi[:, k], w2_lo[:, k])) for k in range(HC)])
                if t % 2:
                    last.then_inc(f2_mm, 1)

            pe.wait_ge(vecs_loaded, 9 * 16)
            pe.wait_ge(w_loaded, 5 * 16)
            n = 0
            for raw, nb, cnt in ((raw_q, 1, G), (raw_kv, 3, G), (raw_w1, 5, HC)):
                for m in range(cnt):
                    for k in range(KC):
                        last = pe.matmul(F[0][:, n:n + 1], raw[:, k, m * P:(m + 1) * P], vecs[:, nb, k:k + 1],
                                         start=(k == 0), stop=(k == KC - 1))
                    n += 1
            last.then_inc(bias_mm, 1)
            for k in range(KC):
                last = pe.matmul(F[1][0:M, 0:C], vecs[:, 3, k:k + 1].to_broadcast([P, M]), raw_kv[:, k, C:],
                                 start=(k == 0), stop=(k == KC - 1))
            last.then_inc(bias_mm, 1)
            pe.wait_ge(setup_done, SETUP)

            cT(0)
            pe.wait_ge(cT_lo_done, 1)
            xT(0, 0)
            pe.wait_ge(xT_lo_done, 1)
            k_proj(0)
            pe.wait_ge(k_step, G)
            xT(0, 1)
            pe.wait_ge(xT_lo_done, 2)
            v_proj(0)
            pe.wait_ge(v_rows_done, 1)
            q_proj(0, 0)
            pe.wait_ge(q_lo_done, 1)
            q_proj(0, 1)
            pe.wait_ge(q_lo_done, 2)

            def body(j, par, mlp, prep):
                scores(j, par, 0)
                scores(j, par, 1)
                if mlp:
                    hT(j - 1, 0)
                    hT(j - 1, 1)
                scores(j, par, 2)
                scores(j, par, 3)
                if mlp:
                    fc1(j - 1, 0)
                    fc1(j - 1, 1)
                pT(j, 0, 0)
                if mlp:
                    fc1(j - 1, 2)
                    fc1(j - 1, 3)
                pT(j, 0, 1)
                pe.wait_ge(q_lo_done, G * (j + 1))
                if prep:
                    cT(j + 1)
                if mlp:
                    fc1(j - 1, 4)
                if prep:
                    pe.wait_ge(cT_lo_done, j + 2)
                    k_proj(j + 1)
                scores(j, par, 4)
                pT(j, 0, 2)
                if prep:
                    pe.wait_ge(k_step, (G + 2) * (j + 1) + G)
                    v_proj(j + 1)
                scores(j, par, 5)
                pT(j, 1, 0)
                if prep:
                    pe.wait_ge(v_rows_done, j + 2)
                else:
                    pe.wait_ge(x1_done, 2 * j)
                attend(j, 0)
                pT(j, 1, 1)
                if mlp:
                    fc1(j - 1, 5)
                scores(j, par, 6)
                if prep:
                    pe.wait_ge(o_scaled, BG * j + 1)
                    xT(j + 1, 0)
                pT(j, 1, 2)
                if mlp:
                    fc1(j - 1, 6)
                pT(j, 2, 0)
                if prep:
                    pe.wait_ge(xT_lo_done, KC * (j + 1) + 1)
                else:
                    pe.wait_ge(o_scaled, BG * j + 1)
                attend(j, 1)
                if mlp:
                    fc1(j - 1, 7)
                if prep:
                    pe.wait_ge(o_scaled, BG * j + 2)
                    xT(j + 1, 1)
                pT(j, 2, 1)
                scores(j, par, 7)
                if prep:
                    pe.wait_ge(xT_lo_done, KC * (j + 2))
                    q_proj(j + 1, 0)
                pT(j, 2, 2)
                if mlp:
                    fc2(j - 1, 0)
                if prep:
                    pe.wait_ge(q_lo_done, G * (j + 1) + 1)
                else:
                    pe.wait_ge(o_scaled, BG * j + 2)
                project(j, 0)
                pT(j, 3, 0)
                pT(j, 3, 1)
                pe.wait_ge(x1_done, 2 * j + 1)
                attend(j, 2)
                pT(j, 3, 2)
                if mlp:
                    fc2(j - 1, 1)
                pe.wait_ge(o_scaled, BG * j + 3)
                attend(j, 3)
                if mlp:
                    fc2(j - 1, 2)
                pe.wait_ge(o_scaled, BG * j + 4)
                project(j, 1)
                if mlp:
                    fc2(j - 1, 3)
                if prep:
                    pe.wait_ge(x1_done, 2 * j + 2)
                    q_proj(j + 1, 1)
            pairs_of(pe, body)
            last_pair = PAIRS - 1
            hT(last_pair, 0)
            hT(last_pair, 1)
            for k in range(HC):
                fc1(last_pair, k)
            for t in range(TT):
                fc2(last_pair, t)


CONSTS = 12
SETUP = 1 + 3 + 8 + 4

_INS = ['x', 'ctx_1024', 'mask_BxSxS2_bk0', 'L0_xattn_qn_w', 'L0_xattn_qn_b', 'L0_xattn_cn_w', 'L0_xattn_cn_b',
        'L0_xattn_n2_w', 'L0_xattn_n2_b', 'L0_xattn_q_w', 'L0_xattn_kv_w', 'L0_xattn_proj_w', 'L0_xattn_proj_b',
        'L0_xattn_fc1_w', 'L0_xattn_fc1_b', 'L0_xattn_fc2_w', 'L0_xattn_fc2_b']


def kernel(**inputs):
    import numpy as _np
    import concourse.bacc as _bacc
    from concourse import mybir as _mybir
    from concourse.bass_utils import run_bass_kernel_spmd as _run

    nc = _bacc.Bacc("TRN2", target_bir_lowering=False, num_devices=1)
    arrays, args = {}, []
    for name in _INS:
        a = _np.ascontiguousarray(inputs[name])
        arrays[f"in_{name}"] = a
        args.append(nc.dram_tensor(f"in_{name}", a.shape, _mybir.dt.from_np(a.dtype), kind="ExternalInput").ap())
    shape = arrays["in_x"].shape
    args.append(nc.dram_tensor("out_0", shape, _mybir.dt.float32, kind="ExternalOutput").ap())
    xattn_block(nc, *args)
    r = _run(nc, [arrays], core_ids=[0])
    return r.results[0]["out_0"]
```

```python
import concourse.bass as bass
from concourse import mybir
from contextlib import ExitStack


def xattn_block(nc, x, ctx, mask, qn_w, qn_b, cn_w, cn_b, n2_w, n2_b, q_w, kv_w, proj_w, proj_b,
                fc1_w, fc1_b, fc2_w, fc2_b, out):
    F32 = mybir.dt.float32
    F32R = mybir.dt.float32r
    BF16 = mybir.dt.bfloat16
    ALU = mybir.AluOpType
    ACT = mybir.ActivationFunctionType
    X = mybir.AxisListType.X

    B, N, C = x.shape
    M = ctx.shape[1]
    HID = fc1_w.shape[1]
    H, D = 16, 16
    P = 128
    EPS = 1e-5
    SCALE = float(D) ** -0.5
    MASKED = -float(2 ** 127)
    NB = 2
    PAIRS = B // NB
    TT = NB * N // P
    KC = C // P
    HC = HID // P
    G = H * D // P
    HG = H // G
    UNITS = TT * G
    BG = NB * G
    MP = -(-M // D) * D
    NM = HG * MP // P
    HM = HG // 2 * M
    TN = TT * P

    es = ExitStack()
    with es:
        def sb(name, shape, dt=F32):
            return es.enter_context(nc.sbuf_tensor(name, shape, dt))

        def sem(name):
            return es.enter_context(nc.semaphore(name))

        qw_hi, qw_lo = sb("qw_hi", [P, KC, C], F32R), sb("qw_lo", [P, KC, C], F32R)
        kvw_hi, kvw_lo = sb("kvw_hi", [P, KC, 2 * C], F32R), sb("kvw_lo", [P, KC, 2 * C], F32R)
        pw_hi, pw_lo = sb("pw_hi", [P, KC, C], F32R), sb("pw_lo", [P, KC, C], F32R)
        w1_hi, w1_lo = sb("w1_hi", [P, KC, HID], F32R), sb("w1_lo", [P, KC, HID], F32R)
        w2_hi, w2_lo = sb("w2_hi", [P, HC, C], F32R), sb("w2_lo", [P, HC, C], F32R)
        vecs = sb("vecs", [P, 6, KC])
        fc1b = sb("fc1b", [P, HC])
        bias = sb("bias", [P, 2 * G + HC])
        bv = sb("bv", [M, C])
        projb = sb("projb", [P, C])
        fc2b = sb("fc2b", [P, C])
        ident = sb("ident", [P, P])
        ident_bf = sb("ident_bf", [P, P], BF16)
        head_of = sb("head_of", [P, HG])
        chunk_head = sb("chunk_head", [P, NM, HG])
        neg_half = sb("neg_half", [P, TT + NB])
        eps = sb("eps", [P, TT + NB])
        NP = 4
        probs = [sb(f"probs{u}", [P, HG, MP]) for u in range(NP)]
        flat = [p[:].rearrange("p h m -> p (h m)") for p in probs]
        probsT = [sb(f"probsT{k}", [P, NM, N]) for k in range(2)]
        g_f = [sb(f"g_f{k}", [P, TN]) for k in range(2)]

        xin = [sb(f"xin{k}", [P, TT, C]) for k in range(2)]
        x1 = [sb(f"x1_{k}", [P, TT, C]) for k in range(2)]
        ctxin = sb("ctxin", [M, NB, C])
        xn = sb("xn", [P, TT, C])
        cn = sb("cn", [M, NB, C])
        stats = sb("stats", [P, TT + NB, 6])
        moms = sb("moms", [P, TT + NB, 2])
        rstd = sb("rstd", [P, TT + NB])
        stats2 = sb("stats2", [P, TT, 6])
        moms2 = sb("moms2", [P, TT, 2])
        rstd2 = sb("rstd2", [P, TT])
        hn = xn
        xT_hi, xT_lo = sb("xT_hi", [P, KC, TN], F32R), sb("xT_lo", [P, KC, TN], F32R)
        hT_hi, hT_lo = sb("hT_hi", [P, KC, TN], F32R), sb("hT_lo", [P, KC, TN], F32R)
        cT_hi, cT_lo = sb("cT_hi", [P, KC, NB * M], F32R), sb("cT_lo", [P, KC, NB * M], F32R)
        q_hi, q_lo = sb("q_hi", [P, G, TN], F32R), sb("q_lo", [P, G, TN], F32R)
        k_hi = sb("k_hi", [P, G, NB, M])
        k_lo = sb("k_lo", [P, G, NB, M])
        kd_hi = sb("kd_hi", [P, BG, HG * M], F32R)
        kd_lo = sb("kd_lo", [P, BG, HG * M], F32R)
        v_rows = sb("v_rows", [MP, NB * C])
        v_rep = sb("v_rep", [P, BG, NM, D])
        vd = sb("vd", [P, BG, NM, HG * D])
        mask_u8 = sb("mask_u8", [P, TT, M], mask.dtype)
        mask_b = [sb(f"mask_b{k}", [P, TT, M], BF16) for k in range(2)]
        rmax = [sb(f"rmax{k}", [P, HG]) for k in range(2)]
        carrier = sb("carrier", [P, 1])
        rsum = sb("rsum", [P, HG])
        rinv = [sb(f"rinv{k}", [P, HG, D]) for k in range(NP)]
        rinvT = sb("rinvT", [P, N])
        o_f = sb("o_f", [P, N])
        oT_hi, oT_lo = sb("oT_hi", [P, G, TN], F32R), sb("oT_lo", [P, G, TN], F32R)
        with ExitStack() as first_user:
            def raw(name, k, n):
                return first_user.enter_context(nc.sbuf_tensor(name, [P, k, n], F32))
            raw_w1, raw_w2 = raw("raw_w1", KC, HID), raw("raw_w2", HC, C)
            raw_q, raw_kv, raw_p = raw("raw_q", KC, C), raw("raw_kv", KC, 2 * C), raw("raw_p", KC, C)
        g_hi, g_lo = sb("g_hi", [P, HC, TN], F32R), sb("g_lo", [P, HC, TN], F32R)

        v_dram = nc.dram_tensor("v_dram", [2, NB * H, MP, D], F32, kind="Internal").ap()

        S = [es.enter_context(nc.psum_tensor(f"S{k}", [P, 2, 512], F32)) for k in range(2)]
        T = es.enter_context(nc.psum_tensor("T", [P, 512], F32))
        Q = es.enter_context(nc.psum_tensor("Q", [P, 512], F32))
        F = [es.enter_context(nc.psum_tensor(f"F{k}", [P, 512], F32)) for k in range(2)]

        consts = sem("consts")
        qkv_loaded = sem("qkv_loaded")
        pw_loaded = sem("pw_loaded")
        mlp_loaded = sem("mlp_loaded")
        vecs_loaded = sem("vecs_loaded")
        bias_mm = sem("bias_mm")
        w_hi_done = sem("w_hi_done")
        setup_done = sem("setup_done")
        x_loaded = sem("x_loaded")
        ctx_loaded = sem("ctx_loaded")
        mask_loaded = sem("mask_loaded")
        mask_ready = sem("mask_ready")
        stats_done = sem("stats_done")
        moms_done = sem("moms_done")
        rstd_step = sem("rstd_step")
        xn_done = sem("xn_done")
        cn_done = sem("cn_done")
        xb_done = sem("xb_done")
        cT_mm = sem("cT_mm")
        cT_hi_done = sem("cT_hi_done")
        cT_lo_done = sem("cT_lo_done")
        xT_mm = sem("xT_mm")
        xT_hi_done = sem("xT_hi_done")
        xT_lo_done = sem("xT_lo_done")
        k_mm = sem("k_mm")
        k_step = sem("k_step")
        kd_done = sem("kd_done")
        v_mm = sem("v_mm")
        v_rows_done = sem("v_rows_done")
        v_stored = sem("v_stored")
        v_gathered = sem("v_gathered")
        vd_done = sem("vd_done")
        q_mm = sem("q_mm")
        q_hi_done = sem("q_hi_done")
        q_lo_done = sem("q_lo_done")
        s_mm = sem("s_mm")
        max_done = sem("max_done")
        shifted = sem("shifted")
        exp_done = sem("exp_done")
        sum_done = sem("sum_done")
        rinv_done = sem("rinv_done")
        pT_mm = sem("pT_mm")
        pT_done = sem("pT_done")
        o_mm = sem("o_mm")
        rinvT_done = sem("rinvT_done")
        o_scaled = sem("o_scaled")
        o_hi_done = sem("o_hi_done")
        o_lo_done = sem("o_lo_done")
        proj_mm = sem("proj_mm")
        x1_done = sem("x1_done")
        stats2_done = sem("stats2_done")
        moms2_done = sem("moms2_done")
        rstd2_step = sem("rstd2_step")
        hn_done = sem("hn_done")
        x1b_done = sem("x1b_done")
        hT_mm = sem("hT_mm")
        hT_hi_done = sem("hT_hi_done")
        hT_lo_done = sem("hT_lo_done")
        f1_mm = sem("f1_mm")
        gelu_done = sem("gelu_done")
        g_hi_done = sem("g_hi_done")
        g_lo_done = sem("g_lo_done")
        f2_mm = sem("f2_mm")
        y_done = sem("y_done")
        y_stored = sem("y_stored")

        def least(n):
            return max(n, 0) if isinstance(n, int) else n

        def mlp_weight_part(n):
            if n < 4:
                k, cols = n // 2, slice(n % 2 * (HID // 2), (n % 2 + 1) * (HID // 2))
                return w1_hi[:, k, cols], w1_lo[:, k, cols], raw_w1[:, k, cols], k
            k = slice(n % 4 * (HC // 4), (n % 4 + 1) * (HC // 4))
            return w2_hi[:, k], w2_lo[:, k], raw_w2[:, k], None

        def min_pair(j):
            return min(j, PAIRS) if isinstance(j, int) else j

        def pairs_of(eng, body):
            body(0, 0, False, True, True)
            body(1, 1, True, True, True)
            with eng.Fori(0, PAIRS // 2 - 2) as i:
                body(2 * i + 2, 0, True, True, True)
                body(2 * i + 3, 1, True, True, True)
            body(PAIRS - 2, 0, True, True, False)
            body(PAIRS - 1, 1, True, False, False)

        block = es.enter_context(nc.Block())

        @block.sync
        def _(sp):
            def load_x(j, par):
                if not isinstance(j, int):
                    sp.wait_ge(consts, CONSTS)
                sp.wait_ge(x1_done, least(2 * (j - 1)))
                sp.dma_start(xin[par][:], x.rearrange("b (t p) c -> p (b t) c", p=P)[:, bass.ts(j, TT), :]).then_inc(x_loaded, 16)

            def load_ctx(j):
                if not isinstance(j, int):
                    sp.wait_ge(consts, CONSTS)
                sp.wait_ge(cn_done, NB * j)
                sp.dma_start(ctxin[:], ctx.rearrange("b m c -> m b c")[:, bass.ts(j, NB), :]).then_inc(ctx_loaded, 16)

            def load_mask(j):
                if not isinstance(j, int):
                    sp.wait_ge(consts, CONSTS)
                sp.wait_ge(mask_ready, j)
                sp.dma_start(mask_u8[:], mask.rearrange("b (t p) m -> p (b t) m", p=P)[:, bass.ts(j, TT), :]).then_inc(mask_loaded, 16)

            def spread_v(j, par):
                sp.wait_ge(v_rows_done, j + 1)
                sp.dma_start(v_dram[par].rearrange("x m d -> m x d"), v_rows[:].rearrange("m (x d) -> m x d", d=D)).then_inc(v_stored, 16)
                sp.wait_ge(v_stored, 16 * (j + 1))
                sp.wait_ge(vd_done, BG * j)
                sp.dma_start(v_rep[:], v_dram[par].rearrange("(g h) m d -> g (h m) d", h=HG)
                             .rearrange("g (c p) d -> p g c d", p=P)).then_inc(v_gathered, 16)

            def store(j, par, half):
                sp.wait_ge(consts, CONSTS)
                sp.wait_ge(y_done, 2 * j + half + 1)
                dst = out.rearrange("b (t p) c -> p (b t) c", p=P)
                sp.dma_start(dst[:, bass.ds(j * TT + half * 2, 2), :], x1[par][:, 2 * half:2 * half + 2]).then_inc(y_stored, 16)

            load_ctx(0)
            load_x(0, 0)
            for dst, src in ((raw_kv, kv_w), (raw_q, q_w)):
                sp.dma_start(dst[:], src.rearrange("(k p) n -> p k n", p=P)).then_inc(qkv_loaded, 16)
            load_mask(0)
            sp.dma_start(raw_p[:], proj_w.rearrange("(k p) n -> p k n", p=P)).then_inc(pw_loaded, 16)
            for dst, src in ((raw_w1, fc1_w), (raw_w2, fc2_w)):
                sp.dma_start(dst[:], src.rearrange("(k p) n -> p k n", p=P)).then_inc(mlp_loaded, 16)
            load_ctx(1)
            spread_v(0, 0)
            load_mask(1)

            def body(j, par, mlp, prep, ahead):
                if prep:
                    load_x(j + 1, 1 - par)
                if ahead:
                    load_ctx(j + 2)
                if prep:
                    spread_v(j + 1, 1 - par)
                if ahead:
                    load_mask(j + 2)
                if mlp:
                    store(j - 1, 1 - par, 0)
                    store(j - 1, 1 - par, 1)
            pairs_of(sp, body)
            store(PAIRS - 1, 1, 0)
            store(PAIRS - 1, 1, 1)
            sp.wait_ge(y_stored, 32 * PAIRS)
            sp.wait_ge(v_stored, 16 * PAIRS)

        @block.gpsimd
        def _(pool):
            pool.memset(ident[:], 0.0).then_inc(consts, 1)
            pool.memset(head_of[:], 1.0).then_inc(consts, 1)
            pool.memset(chunk_head[:], 1.0).then_inc(consts, 1)
            pool.memset(neg_half[:], -0.5).then_inc(consts, 1)
            pool.memset(eps[:], EPS).then_inc(consts, 1)
            pool.memset(v_rows[:], 0.0).then_inc(consts, 1)
            pool.memset(moms[:], 1.0).then_inc(consts, 1)
            pool.wait_ge(consts, 7)
            pool.affine_select(out=ident[:], in_=ident[:], compare_op=ALU.not_equal, fill=1.0, base=0,
                               pattern=[[-1, P]], channel_multiplier=1).then_inc(consts, 1)
            pool.affine_select(out=head_of[:], in_=head_of[:], compare_op=ALU.is_ge, fill=0.0, base=0,
                               pattern=[[-D, HG]], channel_multiplier=1).then_inc(consts, 1)
            pool.affine_select(out=chunk_head[:], in_=chunk_head[:], compare_op=ALU.is_ge, fill=0.0, base=0,
                               pattern=[[P, NM], [-MP, HG]], channel_multiplier=1).then_inc(consts, 1)
            pool.wait_ge(consts, 10)
            pool.affine_select(out=head_of[:], in_=head_of[:], compare_op=ALU.is_ge, fill=0.0, base=D - 1,
                               pattern=[[D, HG]], channel_multiplier=-1).then_inc(consts, 1)
            pool.affine_select(out=chunk_head[:], in_=chunk_head[:], compare_op=ALU.is_ge, fill=0.0, base=MP - 1,
                               pattern=[[-P, NM], [MP, HG]], channel_multiplier=-1).then_inc(consts, 1)
            pool.wait_ge(consts, CONSTS)

            def rstd_x(j):
                pool.wait_ge(xn_done, TT * j)
                pool.wait_ge(cn_done, NB * j)
                pool.wait_ge(moms_done, (TT + NB) * (j + 1))
                pool.tensor_tensor(rstd[:], moms[:, :, 1], eps[:], ALU.add).then_inc(rstd_step, 1)
                pool.wait_ge(rstd_step, 2 * j + 1)
                pool.tensor_tensor(rstd[:], rstd[:], neg_half[:], ALU.pow).then_inc(rstd_step, 1)

            def rstd_h(j):
                pool.wait_ge(hn_done, TT * j)
                pool.wait_ge(moms2_done, TT * (j + 1))
                pool.tensor_tensor(rstd2[:], moms2[:, :, 1], eps[:, 0:TT], ALU.add).then_inc(rstd2_step, 1)
                pool.wait_ge(rstd2_step, 2 * j + 1)
                pool.tensor_tensor(rstd2[:], rstd2[:], neg_half[:, 0:TT], ALU.pow).then_inc(rstd2_step, 1)

            def add_proj_b(j, par):
                pool.wait_ge(xn_done, TT * (j + 1))
                pool.tensor_tensor(xin[par][:], xin[par][:], projb[:].unsqueeze(1).to_broadcast([P, TT, C]),
                                   ALU.add).then_inc(xb_done, 1)

            def add_fc2_b(j, par):
                pool.wait_ge(hn_done, TT * (j + 1))
                pool.tensor_tensor(x1[par][:], x1[par][:], fc2b[:].unsqueeze(1).to_broadcast([P, TT, C]),
                                   ALU.add).then_inc(x1b_done, 1)

            def spread_k(j, bg):
                b, g = divmod(bg, G)
                pool.wait_ge(k_step, (G + 2) * (j + 1))
                pool.wait_ge(s_mm, least(UNITS * (j - 1) + 2 * bg + 2))
                for part, src in ((kd_hi, k_hi), (kd_lo, k_lo)):
                    pool.tensor_tensor(part[:, bg].rearrange("p (h m) -> p h m", m=M),
                                       src[:, g, b].unsqueeze(1).to_broadcast([P, HG, M]),
                                       head_of[:].unsqueeze(2).to_broadcast([P, HG, M]), ALU.mult).then_inc(kd_done, 1)

            def spread_v(j, bg):
                pool.wait_ge(v_gathered, 16 * (j + 1))
                pool.wait_ge(o_mm, least(BG * (j - 1) + bg + 1))
                pool.tensor_tensor(vd[:, bg].rearrange("p c (h d) -> p c h d", d=D),
                                   v_rep[:, bg].unsqueeze(2).to_broadcast([P, NM, HG, D]),
                                   chunk_head[:].unsqueeze(3).to_broadcast([P, NM, HG, D]),
                                   ALU.mult).then_inc(vd_done, 1)

            def low_o(j, bg):
                b, g = divmod(bg, G)
                pool.wait_ge(o_scaled, BG * j + bg + 1)
                pool.wait_ge(o_hi_done, BG * j + bg + 1)
                pool.wait_ge(proj_mm, least(2 * (j - 1) + b + 1))
                cols = slice(b * N, (b + 1) * N)
                pool.tensor_tensor(oT_lo[:, g, cols], o_f[:], oT_hi[:, g, cols].bitcast(F32),
                                   ALU.subtract).then_inc(o_lo_done, 1)

            rstd_x(0)
            pool.wait_ge(vecs_loaded, 9 * 16)
            add_proj_b(0, 0)
            for bg in range(BG):
                spread_k(0, bg)
            for bg in range(BG):
                spread_v(0, bg)

            def body(j, par, mlp, prep, ahead):
                if prep:
                    rstd_x(j + 1)
                low_o(j, 0)
                if mlp:
                    add_fc2_b(j - 1, 1 - par)
                if prep:
                    spread_k(j + 1, 0)
                    add_proj_b(j + 1, 1 - par)
                    spread_v(j + 1, 0)
                low_o(j, 1)
                if prep:
                    spread_k(j + 1, 1)
                    spread_v(j + 1, 1)
                    spread_k(j + 1, 2)
                    spread_k(j + 1, 3)
                low_o(j, 2)
                if prep:
                    spread_v(j + 1, 2)
                low_o(j, 3)
                if prep:
                    spread_v(j + 1, 3)
                rstd_h(j)
            pairs_of(pool, body)
            add_fc2_b(PAIRS - 1, 1)

        @block.scalar
        def _(act):
            for k, v in enumerate((qn_w, qn_b, cn_w, cn_b, n2_w, n2_b)):
                act.dma_start(vecs[:, k], v.rearrange("(k p) -> p k", p=P), allow_slow_non_contiguous=True).then_inc(vecs_loaded, 16)
            act.dma_start(fc1b[:], fc1_b.rearrange("(k p) -> p k", p=P), allow_slow_non_contiguous=True).then_inc(vecs_loaded, 16)
            act.dma_start(projb[:], proj_b.unsqueeze(0).to_broadcast([P, C])).then_inc(vecs_loaded, 16)
            act.dma_start(fc2b[:], fc2_b.unsqueeze(0).to_broadcast([P, C])).then_inc(vecs_loaded, 16)
            act.wait_ge(vecs_loaded, 9 * 16)
            act.wait_ge(qkv_loaded, 2 * 16)
            for hi, raw, nw in ((kvw_hi, raw_kv, 2), (qw_hi, raw_q, 0)):
                for k in range(KC):
                    act.activation(hi[:, k], raw[:, k], ACT.Copy, scale=vecs[:, nw, k:k + 1]).then_inc(w_hi_done, 1)

            def proj_weight_high():
                act.wait_ge(pw_loaded, 16)
                act.activation(pw_hi[:], raw_p[:], ACT.Copy).then_inc(w_hi_done, 1)

            def mlp_weight_high(n):
                act.wait_ge(mlp_loaded, 2 * 16)
                hi, _, raw, k = mlp_weight_part(n)
                if n < 4:
                    act.activation(hi, raw, ACT.Copy, scale=vecs[:, 4, k:k + 1]).then_inc(w_hi_done, 1)
                else:
                    act.activation(hi, raw, ACT.Copy).then_inc(w_hi_done, 1)

            def cT_high(j):
                act.wait_ge(cT_mm, j + 1)
                act.wait_ge(k_mm, j)
                act.wait_ge(v_mm, j)
                act.activation(cT_hi[:].rearrange("p k (b m) -> p k b m", m=M),
                               Q[:, 0:KC * NB * MP].rearrange("p (k b m) -> p k b m", k=KC, m=MP)[:, :, :, 0:M],
                               ACT.Copy).then_inc(cT_hi_done, 1)

            def xT_high(j, k):
                act.wait_ge(xT_mm, KC * j + k + 1)
                act.wait_ge(q_mm, G * j)
                act.activation(xT_hi[:, k], Q[:], ACT.Copy).then_inc(xT_hi_done, 1)

            def q_high(j, g):
                act.wait_ge(q_mm, G * j + g + 1)
                act.wait_ge(s_mm, least(UNITS * (j - 1) + 6 + 2 * g))
                act.activation(q_hi[:, g], Q[:], ACT.Identity, bias=bias[:, g:g + 1]).then_inc(q_hi_done, 1)

            def exp(j, u):
                act.wait_ge(shifted, UNITS * j + u + 1)
                act.activation(probs[u % NP][:, :, 0:M], probs[u % NP][:, :, 0:M], ACT.Exp, scale=SCALE).then_inc(exp_done, 1)

            def pT_copy(j, bg, s):
                n = 1 if s == 2 else 2
                act.wait_ge(pT_mm, 3 * (BG * j + bg) + s + 1)
                act.wait_ge(o_mm, least(BG * j + bg - 1))
                act.activation(probsT[bg % 2][:, 2 * s:2 * s + n], T[:, 0:n * N].rearrange("p (c n) -> p c n", n=N),
                               ACT.Copy).then_inc(pT_done, 1)

            def rinvT_copy(j, bg):
                act.wait_ge(o_mm, BG * j + bg + 1)
                act.wait_ge(o_scaled, BG * j + bg)
                act.activation(rinvT[:], Q[:, N:2 * N], ACT.Copy).then_inc(rinvT_done, 1)

            def hT_high(j, k):
                act.wait_ge(setup_done, ALL_READY)
                act.wait_ge(hT_mm, KC * j + k + 1)
                act.wait_ge(f1_mm, HC * j)
                act.activation(hT_hi[:, k], F[k][:], ACT.Copy).then_inc(hT_hi_done, 1)

            def gelu(j, k):
                act.wait_ge(f1_mm, HC * j + k + 1)
                act.wait_ge(g_lo_done, least(HC * j + max(k - 1, 0)))
                act.wait_ge(f2_mm, 2 * j)
                b1 = bias[:, 2 * G + k:2 * G + k + 1]
                act.activation(g_f[k % 2][:], F[k % 2][:], ACT.Gelu, bias=b1).then_inc(gelu_done, 1)
                act.activation(g_hi[:, k], F[k % 2][:], ACT.Gelu, bias=b1).then_inc(g_hi_done, 1)

            cT_high(0)
            xT_high(0, 0)
            xT_high(0, 1)
            act.wait_ge(setup_done, QKV_READY)
            q_high(0, 0)
            q_high(0, 1)
            exp(0, 0)
            exp(0, 1)
            exp(0, 2)
            pT_copy(0, 0, 0)

            def body(j, par, mlp, prep, ahead):
                pT_copy(j, 0, 1)
                pT_copy(j, 0, 2)
                if mlp:
                    hT_high(j - 1, 0)
                else:
                    proj_weight_high()
                if mlp:
                    hT_high(j - 1, 1)
                exp(j, 3)
                rinvT_copy(j, 0)
                if mlp:
                    gelu(j - 1, 0)
                else:
                    mlp_weight_high(0)
                pT_copy(j, 1, 0)
                if mlp:
                    gelu(j - 1, 1)
                else:
                    mlp_weight_high(1)
                if prep:
                    cT_high(j + 1)
                pT_copy(j, 1, 1)
                if mlp:
                    gelu(j - 1, 2)
                else:
                    mlp_weight_high(2)
                exp(j, 4)
                exp(j, 5)
                if mlp:
                    gelu(j - 1, 3)
                else:
                    mlp_weight_high(3)
                if prep:
                    xT_high(j + 1, 0)
                pT_copy(j, 1, 2)
                if mlp:
                    gelu(j - 1, 4)
                else:
                    mlp_weight_high(4)
                if prep:
                    xT_high(j + 1, 1)
                if mlp:
                    gelu(j - 1, 5)
                else:
                    mlp_weight_high(5)
                pT_copy(j, 2, 0)
                if prep:
                    q_high(j + 1, 0)
                if mlp:
                    gelu(j - 1, 6)
                else:
                    mlp_weight_high(6)
                pT_copy(j, 2, 1)
                if mlp:
                    gelu(j - 1, 7)
                else:
                    mlp_weight_high(7)
                rinvT_copy(j, 1)
                exp(j, 6)
                exp(j, 7)
                pT_copy(j, 2, 2)
                if prep:
                    q_high(j + 1, 1)
                pT_copy(j, 3, 0)
                pT_copy(j, 3, 1)
                if prep:
                    exp(j + 1, 0)
                rinvT_copy(j, 2)
                pT_copy(j, 3, 2)
                if prep:
                    exp(j + 1, 1)
                rinvT_copy(j, 3)
                if prep:
                    exp(j + 1, 2)
                    pT_copy(j + 1, 0, 0)
            pairs_of(act, body)
            hT_high(PAIRS - 1, 0)
            hT_high(PAIRS - 1, 1)
            for k in range(HC):
                gelu(PAIRS - 1, k)

        @block.vector
        def _(dve):
            def low(dst, src, hi):
                return dve.tensor_tensor(dst, src, hi.bitcast(F32), ALU.subtract)

            def ln_stats(j, par):
                dve.wait_ge(rstd_step, 2 * j)
                dve.wait_ge(x_loaded, 16 * (j + 1))
                for t in range(TT):
                    dve.bn_stats(stats[:, t], xin[par][:, t]).then_inc(stats_done, 1)
                dve.wait_ge(ctx_loaded, 16 * (j + 1))
                for b in range(NB):
                    dve.bn_stats(stats[0:M, TT + b], ctxin[:, b]).then_inc(stats_done, 1)

            def ln_moments(j):
                dve.wait_ge(stats_done, (TT + NB) * (j + 1))
                dve.memset(carrier[:], 0.0)
                for t in range(TT):
                    dve.bn_aggr(moms[:, t], stats[:, t]).then_inc(moms_done, 1)
                for b in range(NB):
                    dve.bn_aggr(moms[0:M, TT + b], stats[0:M, TT + b]).then_inc(moms_done, 1)

            def normalise_ctx(j):
                dve.wait_ge(rstd_step, 2 * (j + 1))
                dve.wait_ge(cT_mm, j)
                for b in range(NB):
                    dve.tensor_scalar(cn[:, b], ctxin[:, b], moms[0:M, TT + b, 0:1], rstd[0:M, TT + b:TT + b + 1],
                                      ALU.subtract, ALU.mult).then_inc(cn_done, 1)

            def normalise_x(j, par):
                dve.wait_ge(rstd_step, 2 * (j + 1))
                dve.wait_ge(hT_mm, least(KC * (j - 1)))
                for t in range(TT):
                    dve.tensor_scalar(xn[:, t], xin[par][:, t], moms[:, t, 0:1], rstd[:, t:t + 1],
                                      ALU.subtract, ALU.mult).then_inc(xn_done, 1)

            def mask_bias(j, par):
                dve.wait_ge(mask_loaded, 16 * (j + 1))
                dve.wait_ge(s_mm, least(UNITS * (j - 1)))
                dve.tensor_scalar(mask_b[par][:], mask_u8[:], MASKED, None, ALU.mult).then_inc(mask_ready, 1)

            def cT_low(j):
                dve.wait_ge(cT_hi_done, j + 1)
                low(cT_lo[:].rearrange("p k (b m) -> p k b m", m=M),
                    Q[:, 0:KC * NB * MP].rearrange("p (k b m) -> p k b m", k=KC, m=MP)[:, :, :, 0:M],
                    cT_hi[:].rearrange("p k (b m) -> p k b m", m=M)).then_inc(cT_lo_done, 1)

            def xT_low(j, k):
                dve.wait_ge(xT_hi_done, KC * j + k + 1)
                low(xT_lo[:, k], Q[:], xT_hi[:, k]).then_inc(xT_lo_done, 1)

            def k_evacuate(j):
                dve.wait_ge(k_mm, j + 1)
                dve.wait_ge(kd_done, 2 * BG * j)
                for g in range(G):
                    dve.tensor_scalar(k_lo[:, g].rearrange("p b m -> p (b m)"), Q[:, g * NB * M:(g + 1) * NB * M],
                                      bias[:, G + g:G + g + 1], None, ALU.add).then_inc(k_step, 1)

            def k_split(j):
                dve.wait_ge(k_step, (G + 2) * j + G)
                dve.tensor_copy(k_hi[:].bitcast(F32R), k_lo[:]).then_inc(k_step, 1)
                dve.wait_ge(k_step, (G + 2) * j + G + 1)
                dve.tensor_tensor(k_lo[:], k_lo[:], k_hi[:], ALU.subtract).then_inc(k_step, 1)

            def v_evacuate(j):
                dve.wait_ge(v_mm, j + 1)
                dve.wait_ge(v_stored, 16 * j)
                dve.tensor_tensor(v_rows[0:M].rearrange("p (b c) -> p b c", c=C), Q[0:M, :].rearrange("p (b c) -> p b c", c=C),
                                  bv[:].unsqueeze(1).to_broadcast([M, NB, C]), ALU.add).then_inc(v_rows_done, 1)

            def q_low(j, g):
                dve.wait_ge(q_hi_done, G * j + g + 1)
                dve.scalar_tensor_tensor(out=q_lo[:, g], in0=Q[:], scalar=bias[:, g:g + 1],
                                         in1=q_hi[:, g].bitcast(F32), op0=ALU.add, op1=ALU.subtract).then_inc(q_lo_done, 1)

            def unit_views(u):
                return (S[u % 2][:, :, 0:HM].rearrange("p a (h m) -> p a h m", m=M),
                        rmax[u % 2][:].rearrange("p (a h) -> p a h", a=2))

            def row_max(j, u):
                sc, mx = unit_views(u)
                dve.wait_ge(s_mm, UNITS * j + u + 1)
                dve.wait_ge(shifted, least(UNITS * j + u - 1))
                dve.tensor_reduce(mx, sc, X, ALU.max).then_inc(max_done, 1)

            def shift(j, u):
                sc, mx = unit_views(u)
                dve.wait_ge(max_done, UNITS * j + u + 1)
                dve.wait_ge(pT_mm, least(3 * (BG * j + (u - NP) // 2 + 1)))
                dve.tensor_tensor(probs[u % NP][:, :, 0:M].rearrange("p (a h) m -> p a h m", a=2), sc,
                                  mx.unsqueeze(3).to_broadcast([P, 2, HG // 2, M]), ALU.subtract).then_inc(shifted, 1)

            def row_sum(j, u):
                dve.wait_ge(exp_done, UNITS * j + u + 1)
                dve.wait_ge(rinv_done, UNITS * j + u)
                dve.tensor_reduce(rsum[:], probs[u % NP][:, :, 0:M], X, ALU.add).then_inc(sum_done, 1)
                dve.wait_ge(sum_done, 2 * (UNITS * j + u) + 1)
                dve.wait_ge(o_mm, least(BG * j + (u - NP) // 2 + 1))
                dve.reciprocal(rsum[:], rsum[:]).then_inc(sum_done, 1)
                dve.wait_ge(sum_done, 2 * (UNITS * j + u + 1))
                dve.tensor_copy(rinv[u % NP][:], rsum[:].unsqueeze(2).to_broadcast([P, HG, D])).then_inc(rinv_done, 1)

            def o_scale(j, bg):
                dve.wait_ge(rinvT_done, BG * j + bg + 1)
                b, g = divmod(bg, G)
                dve.wait_ge(proj_mm, least(2 * (j - 1) + b + 1))
                dve.tensor_tensor(oT_hi[:, g, b * N:(b + 1) * N], Q[:, 0:N], rinvT[:], ALU.mult).then_inc(o_hi_done, 1)
                dve.wait_ge(o_lo_done, BG * j + bg)
                dve.tensor_tensor(o_f[:], Q[:, 0:N], rinvT[:], ALU.mult).then_inc(o_scaled, 1)

            def add_x(j, par, half):
                dve.wait_ge(proj_mm, 2 * j + half + 1)
                dve.wait_ge(xb_done, j + 1)
                dve.wait_ge(y_stored, least(32 * (j - 1)))
                dve.tensor_tensor(x1[par][:, 2 * half:2 * half + 2], Q[:].rearrange("p (t c) -> p t c", c=C),
                                  xin[par][:, 2 * half:2 * half + 2], ALU.add).then_inc(x1_done, 1)

            def h_stats(j, par, half):
                dve.wait_ge(x1_done, 2 * j + half + 1)
                dve.wait_ge(rstd2_step, 2 * j)
                for t in (2 * half, 2 * half + 1):
                    dve.bn_stats(stats2[:, t], x1[par][:, t]).then_inc(stats2_done, 1)

            def h_moments(j):
                dve.wait_ge(stats2_done, TT * (j + 1))
                dve.memset(carrier[:], 0.0)
                for t in range(TT):
                    dve.bn_aggr(moms2[:, t], stats2[:, t]).then_inc(moms2_done, 1)

            def h_normalise(j, par):
                dve.wait_ge(rstd2_step, 2 * (j + 1))
                dve.wait_ge(xT_mm, KC * min_pair(j + 2))
                for t in range(TT):
                    dve.tensor_scalar(hn[:, t], x1[par][:, t], moms2[:, t, 0:1], rstd2[:, t:t + 1],
                                      ALU.subtract, ALU.mult).then_inc(hn_done, 1)

            def hT_low(j, k):
                dve.wait_ge(hT_hi_done, KC * j + k + 1)
                low(hT_lo[:, k], F[k][:], hT_hi[:, k]).then_inc(hT_lo_done, 1)

            def g_low(j, k):
                dve.wait_ge(gelu_done, HC * j + k + 1)
                dve.wait_ge(g_hi_done, HC * j + k + 1)
                low(g_lo[:, k], g_f[k % 2][:], g_hi[:, k]).then_inc(g_lo_done, 1)

            def add_x1(j, par, half):
                dve.wait_ge(f2_mm, 2 * j + half + 1)
                dve.wait_ge(x1b_done, j + 1)
                dve.tensor_tensor(x1[par][:, 2 * half:2 * half + 2], F[half][:].rearrange("p (t c) -> p t c", c=C),
                                  x1[par][:, 2 * half:2 * half + 2], ALU.add).then_inc(y_done, 1)

            def weight_low(lo, raw, hi, nw, k, n):
                dve.wait_ge(w_hi_done, n)
                dve.scalar_tensor_tensor(out=lo, in0=raw, scalar=vecs[:, nw, k:k + 1], in1=hi.bitcast(F32),
                                         op0=ALU.mult, op1=ALU.subtract).then_inc(setup_done, 1)

            def proj_weight_low():
                dve.wait_ge(w_hi_done, 2 * KC + 1)
                low(pw_lo[:], raw_p[:], pw_hi[:]).then_inc(setup_done, 1)

            def mlp_weight_low(n):
                hi, lo, raw, k = mlp_weight_part(n)
                if n < 4:
                    weight_low(lo, raw, hi, 4, k, 2 * KC + 1 + n + 1)
                else:
                    dve.wait_ge(w_hi_done, 2 * KC + 1 + n + 1)
                    low(lo, raw, hi).then_inc(setup_done, 1)

            def fc1_bias_evacuate():
                dve.wait_ge(bias_mm, 3)
                dve.tensor_tensor(bias[:, 2 * G:], F[0][:, 2 * G:2 * G + HC], fc1b[:], ALU.add).then_inc(setup_done, 1)

            for u in range(NP):
                dve.memset(probs[u][:], 0.0).then_inc(setup_done, 1)
            dve.wait_ge(consts, CONSTS)
            dve.tensor_copy(ident_bf[:], ident[:]).then_inc(setup_done, 1)
            ln_stats(0, 0)
            ln_moments(0)
            normalise_ctx(0)
            normalise_x(0, 0)
            for k in range(KC):
                weight_low(kvw_lo[:, k], raw_kv[:, k], kvw_hi[:, k], 2, k, k + 1)
            cT_low(0)
            for k in range(KC):
                weight_low(qw_lo[:, k], raw_q[:, k], qw_hi[:, k], 0, k, KC + k + 1)
            xT_low(0, 0)
            dve.wait_ge(bias_mm, 2)
            dve.tensor_copy(bias[:, 0:2 * G], F[0][:, 0:2 * G]).then_inc(setup_done, 1)
            dve.tensor_copy(bv[:], F[1][0:M, 0:C]).then_inc(setup_done, 1)
            dve.wait_ge(setup_done, QKV_READY)
            k_evacuate(0)
            xT_low(0, 1)
            k_split(0)
            v_evacuate(0)
            q_low(0, 0)
            mask_bias(0, 0)
            q_low(0, 1)
            row_max(0, 0)
            shift(0, 0)
            row_max(0, 1)
            shift(0, 1)
            row_max(0, 2)
            shift(0, 2)
            row_sum(0, 0)

            def body(j, par, mlp, prep, ahead):
                if mlp:
                    h_normalise(j - 1, 1 - par)
                row_sum(j, 1)
                row_max(j, 3)
                if mlp:
                    hT_low(j - 1, 0)
                else:
                    proj_weight_low()
                shift(j, 3)
                if mlp:
                    hT_low(j - 1, 1)
                if prep:
                    ln_stats(j + 1, 1 - par)
                    ln_moments(j + 1)
                row_max(j, 4)
                o_scale(j, 0)
                if mlp:
                    g_low(j - 1, 0)
                else:
                    mlp_weight_low(0)
                if prep:
                    normalise_ctx(j + 1)
                row_max(j, 5)
                shift(j, 4)
                if prep:
                    cT_low(j + 1)
                shift(j, 5)
                if prep:
                    normalise_x(j + 1, 1 - par)
                    v_evacuate(j + 1)
                if mlp:
                    g_low(j - 1, 1)
                else:
                    mlp_weight_low(1)
                if mlp:
                    g_low(j - 1, 2)
                else:
                    mlp_weight_low(2)
                if prep:
                    k_evacuate(j + 1)
                row_max(j, 6)
                row_sum(j, 2)
                if prep:
                    xT_low(j + 1, 0)
                    k_split(j + 1)
                if mlp:
                    g_low(j - 1, 3)
                else:
                    mlp_weight_low(3)
                if prep:
                    xT_low(j + 1, 1)
                    mask_bias(j + 1, 1 - par)
                row_sum(j, 3)
                if mlp:
                    g_low(j - 1, 4)
                else:
                    mlp_weight_low(4)
                if prep:
                    q_low(j + 1, 0)
                if mlp:
                    g_low(j - 1, 5)
                else:
                    mlp_weight_low(5)
                row_max(j, 7)
                shift(j, 6)
                shift(j, 7)
                o_scale(j, 1)
                row_sum(j, 4)
                if mlp:
                    g_low(j - 1, 6)
                else:
                    mlp_weight_low(6)
                if mlp:
                    g_low(j - 1, 7)
                else:
                    mlp_weight_low(7)
                row_sum(j, 5)
                if prep:
                    q_low(j + 1, 1)
                    row_max(j + 1, 0)
                    shift(j + 1, 0)
                row_sum(j, 6)
                add_x(j, par, 0)
                if prep:
                    row_max(j + 1, 1)
                row_sum(j, 7)
                if prep:
                    shift(j + 1, 1)
                h_stats(j, par, 0)
                if prep:
                    row_max(j + 1, 2)
                o_scale(j, 2)
                if mlp:
                    add_x1(j - 1, 1 - par, 0)
                else:
                    fc1_bias_evacuate()
                o_scale(j, 3)
                if prep:
                    shift(j + 1, 2)
                    row_sum(j + 1, 0)
                add_x(j, par, 1)
                h_stats(j, par, 1)
                h_moments(j)
                if mlp:
                    add_x1(j - 1, 1 - par, 1)
            pairs_of(dve, body)
            h_normalise(PAIRS - 1, 1)
            hT_low(PAIRS - 1, 0)
            hT_low(PAIRS - 1, 1)
            for k in range(HC):
                g_low(PAIRS - 1, k)
            add_x1(PAIRS - 1, 1, 0)
            add_x1(PAIRS - 1, 1, 1)

        @block.tensor
        def _(pe):
            def product(dst, terms, inc=None):
                n = 0
                for (a_hi, a_lo), (b_hi, b_lo) in terms:
                    for a, b in ((a_hi, b_hi), (a_hi, b_lo), (a_lo, b_hi)):
                        last = pe.matmul(dst, a, b, start=(n == 0), stop=(n == 3 * len(terms) - 1))
                        n += 1
                return last

            def cT(j):
                pe.wait_ge(cn_done, NB * (j + 1))
                for k in range(KC):
                    for b in range(NB):
                        at = (k * NB + b) * MP
                        last = pe.transpose(Q[:, at:at + M], cn[:, b, k * P:(k + 1) * P], ident[0:M, 0:M])
                last.then_inc(cT_mm, 1)

            def xT(j, k):
                pe.wait_ge(xn_done, TT * (j + 1))
                for t in range(TT):
                    last = pe.transpose(Q[:, t * P:(t + 1) * P], xn[:, t, k * P:(k + 1) * P], ident[:])
                last.then_inc(xT_mm, 1)

            def k_proj(j):
                pe.wait_ge(cT_lo_done, j + 1)
                for g in range(G):
                    cols = slice(g * P, (g + 1) * P)
                    last = product(Q[:, g * NB * M:(g + 1) * NB * M],
                                   [((kvw_hi[:, k, cols], kvw_lo[:, k, cols]), (cT_hi[:, k], cT_lo[:, k])) for k in range(KC)])
                last.then_inc(k_mm, 1)

            def v_proj(j):
                for b in range(NB):
                    rows = slice(b * M, (b + 1) * M)
                    last = product(Q[0:M, b * C:(b + 1) * C],
                                   [((cT_hi[:, k, rows], cT_lo[:, k, rows]), (kvw_hi[:, k, C:], kvw_lo[:, k, C:])) for k in range(KC)])
                last.then_inc(v_mm, 1)

            def q_proj(j, g):
                pe.wait_ge(xT_lo_done, KC * (j + 1))
                cols = slice(g * P, (g + 1) * P)
                product(Q[:], [((qw_hi[:, k, cols], qw_lo[:, k, cols]), (xT_hi[:, k], xT_lo[:, k]))
                               for k in range(KC)]).then_inc(q_mm, 1)

            def scores(j, par, u):
                bg, t = divmod(u, 2)
                b, g = divmod(bg, G)
                tok = slice((2 * b + t) * P, (2 * b + t + 1) * P)
                pe.wait_ge(q_lo_done, G * j + g + 1)
                pe.wait_ge(kd_done, 2 * (BG * j + bg + 1))
                pe.wait_ge(mask_ready, j + 1)
                pe.wait_ge(shifted, least(UNITS * j + u - 1))
                for a in range(2):
                    dst = S[u % 2][:, a, 0:HM]
                    cols = slice(a * HM, (a + 1) * HM)
                    pe.matmul(dst.rearrange("p (h m) -> p h m", m=M), ident_bf[:],
                              mask_b[par][:, 2 * b + t].unsqueeze(1).to_broadcast([P, HG // 2, M]), start=True, stop=False)
                    pe.matmul(dst, q_hi[:, g, tok], kd_hi[:, bg, cols], start=False, stop=False)
                    pe.matmul(dst, q_hi[:, g, tok], kd_lo[:, bg, cols], start=False, stop=False)
                    last = pe.matmul(dst, q_lo[:, g, tok], kd_hi[:, bg, cols], start=False, stop=True)
                last.then_inc(s_mm, 1)

            def pT(j, bg, s):
                pe.wait_ge(exp_done, UNITS * j + 2 * bg + 2)
                pe.wait_ge(pT_done, 3 * (BG * j + bg) + s)
                for c in range(2 * s, min(2 * s + 2, NM)):
                    for t in range(2):
                        at = (c % 2) * N + t * P
                        last = pe.transpose(T[:, at:at + P], flat[(2 * bg + t) % NP][:, c * P:(c + 1) * P], ident[:])
                last.then_inc(pT_mm, 1)

            def attend(j, bg):
                pe.wait_ge(rinv_done, UNITS * j + 2 * bg + 2)
                for t in range(2):
                    pe.transpose(Q[:, N + t * P:N + (t + 1) * P],
                                 rinv[(2 * bg + t) % NP][:].rearrange("p h d -> p (h d)"), ident[:])
                pe.wait_ge(vd_done, BG * j + bg + 1)
                pe.wait_ge(pT_done, 3 * (BG * j + bg) + 3)
                for c in range(NM):
                    last = pe.matmul(Q[:, 0:N], vd[:, bg, c], probsT[bg % 2][:, c], start=(c == 0), stop=(c == NM - 1))
                last.then_inc(o_mm, 1)

            def project(j, half):
                pe.wait_ge(setup_done, QKV_READY + 1)
                pe.wait_ge(o_lo_done, BG * j + 2 * half + 2)
                for t in (2 * half, 2 * half + 1):
                    tok = slice(t * P, (t + 1) * P)
                    last = product(Q[:, (t % 2) * C:(t % 2 + 1) * C],
                                   [((oT_hi[:, g, tok], oT_lo[:, g, tok]), (pw_hi[:, g], pw_lo[:, g])) for g in range(G)])
                last.then_inc(proj_mm, 1)

            def hT(j, k):
                pe.wait_ge(setup_done, ALL_READY)
                pe.wait_ge(hn_done, TT * (j + 1))
                pe.wait_ge(y_done, 2 * j)
                for t in range(TT):
                    last = pe.transpose(F[k][:, t * P:(t + 1) * P], hn[:, t, k * P:(k + 1) * P], ident[:])
                last.then_inc(hT_mm, 1)

            def fc1(j, k):
                pe.wait_ge(hT_lo_done, KC * (j + 1))
                if k >= 2:
                    pe.wait_ge(g_hi_done, least(HC * j + k - 1))
                cols = slice(k * P, (k + 1) * P)
                product(F[k % 2][:], [((w1_hi[:, c, cols], w1_lo[:, c, cols]), (hT_hi[:, c], hT_lo[:, c]))
                                      for c in range(KC)]).then_inc(f1_mm, 1)

            def fc2(j, t):
                pe.wait_ge(g_hi_done, HC * j + 7 + t // 2)
                pe.wait_ge(g_lo_done, HC * (j + 1))
                tok = slice(t * P, (t + 1) * P)
                last = product(F[t // 2][:, (t % 2) * C:(t % 2 + 1) * C],
                               [((g_hi[:, k, tok], g_lo[:, k, tok]), (w2_hi[:, k], w2_lo[:, k])) for k in range(HC)])
                if t % 2:
                    last.then_inc(f2_mm, 1)

            def bias_columns(raw, nb, at, cnt):
                for m in range(cnt):
                    for k in range(KC):
                        last = pe.matmul(F[0][:, at + m:at + m + 1], raw[:, k, m * P:(m + 1) * P], vecs[:, nb, k:k + 1],
                                         start=(k == 0), stop=(k == KC - 1))
                return last

            def fc1_bias():
                pe.wait_ge(mlp_loaded, 2 * 16)
                bias_columns(raw_w1, 5, 2 * G, HC).then_inc(bias_mm, 1)

            pe.wait_ge(consts, CONSTS)
            cT(0)
            pe.wait_ge(vecs_loaded, 9 * 16)
            pe.wait_ge(qkv_loaded, 2 * 16)
            bias_columns(raw_q, 1, 0, G)
            bias_columns(raw_kv, 3, G, G).then_inc(bias_mm, 1)
            for k in range(KC):
                last = pe.matmul(F[1][0:M, 0:C], vecs[:, 3, k:k + 1].to_broadcast([P, M]), raw_kv[:, k, C:],
                                 start=(k == 0), stop=(k == KC - 1))
            last.then_inc(bias_mm, 1)

            pe.wait_ge(cT_lo_done, 1)
            xT(0, 0)
            pe.wait_ge(xT_lo_done, 1)
            pe.wait_ge(setup_done, QKV_READY)
            k_proj(0)
            pe.wait_ge(k_step, G)
            xT(0, 1)
            pe.wait_ge(xT_lo_done, 2)
            v_proj(0)
            pe.wait_ge(v_rows_done, 1)
            q_proj(0, 0)
            pe.wait_ge(q_lo_done, 1)
            q_proj(0, 1)
            pe.wait_ge(q_lo_done, 2)
            scores(0, 0, 0)
            scores(0, 0, 1)
            scores(0, 0, 2)
            pT(0, 0, 0)
            scores(0, 0, 3)

            def body(j, par, mlp, prep, ahead):
                pT(j, 0, 1)
                scores(j, par, 4)
                pT(j, 0, 2)
                if mlp:
                    hT(j - 1, 0)
                    hT(j - 1, 1)
                pe.wait_ge(x1_done, 2 * j)
                attend(j, 0)
                scores(j, par, 5)
                if mlp:
                    fc1(j - 1, 0)
                else:
                    fc1_bias()
                if mlp:
                    fc1(j - 1, 1)
                pT(j, 1, 0)
                if mlp:
                    fc1(j - 1, 2)
                pT(j, 1, 1)
                if prep:
                    pe.wait_ge(o_scaled, BG * j + 1)
                    cT(j + 1)
                if mlp:
                    fc1(j - 1, 3)
                if prep:
                    pe.wait_ge(cT_lo_done, j + 2)
                    v_proj(j + 1)
                pT(j, 1, 2)
                scores(j, par, 6)
                if prep:
                    pe.wait_ge(v_rows_done, j + 2)
                    k_proj(j + 1)
                if mlp:
                    fc1(j - 1, 4)
                if prep:
                    pe.wait_ge(k_step, (G + 2) * (j + 1) + G)
                    xT(j + 1, 0)
                scores(j, par, 7)
                if mlp:
                    fc1(j - 1, 5)
                if prep:
                    pe.wait_ge(xT_lo_done, KC * (j + 1) + 1)
                    xT(j + 1, 1)
                pT(j, 2, 0)
                if mlp:
                    fc1(j - 1, 6)
                if prep:
                    pe.wait_ge(xT_lo_done, KC * (j + 2))
                    q_proj(j + 1, 0)
                if mlp:
                    fc1(j - 1, 7)
                pT(j, 2, 1)
                if prep:
                    pe.wait_ge(q_lo_done, G * (j + 1) + 1)
                else:
                    pe.wait_ge(o_scaled, BG * j + 1)
                attend(j, 1)
                if prep:
                    scores(j + 1, 1 - par, 0)
                pT(j, 2, 2)
                if prep:
                    scores(j + 1, 1 - par, 1)
                    pe.wait_ge(o_scaled, BG * j + 2)
                    q_proj(j + 1, 1)
                pT(j, 3, 0)
                if mlp:
                    fc2(j - 1, 0)
                pT(j, 3, 1)
                if prep:
                    pe.wait_ge(q_lo_done, G * (j + 2))
                else:
                    pe.wait_ge(o_scaled, BG * j + 2)
                project(j, 0)
                if prep:
                    scores(j + 1, 1 - par, 2)
                pe.wait_ge(x1_done, 2 * j + 1)
                attend(j, 2)
                pT(j, 3, 2)
                if mlp:
                    fc2(j - 1, 1)
                pe.wait_ge(o_scaled, BG * j + 3)
                attend(j, 3)
                if mlp:
                    fc2(j - 1, 2)
                pe.wait_ge(o_scaled, BG * j + 4)
                project(j, 1)
                if mlp:
                    fc2(j - 1, 3)
                if prep:
                    pT(j + 1, 0, 0)
                    scores(j + 1, 1 - par, 3)
            pairs_of(pe, body)
            last_pair = PAIRS - 1
            hT(last_pair, 0)
            hT(last_pair, 1)
            for k in range(HC):
                fc1(last_pair, k)
            for t in range(TT):
                fc2(last_pair, t)


CONSTS = 12
QKV_READY = 4 + 1 + 4 + 2
ALL_READY = QKV_READY + 1 + 8 + 1

_INS = ['x', 'ctx_1024', 'mask_BxSxS2_bk0', 'L0_xattn_qn_w', 'L0_xattn_qn_b', 'L0_xattn_cn_w', 'L0_xattn_cn_b',
        'L0_xattn_n2_w', 'L0_xattn_n2_b', 'L0_xattn_q_w', 'L0_xattn_kv_w', 'L0_xattn_proj_w', 'L0_xattn_proj_b',
        'L0_xattn_fc1_w', 'L0_xattn_fc1_b', 'L0_xattn_fc2_w', 'L0_xattn_fc2_b']


def kernel(**inputs):
    import numpy as _np
    import concourse.bacc as _bacc
    from concourse import mybir as _mybir
    from concourse.bass_utils import run_bass_kernel_spmd as _run

    nc = _bacc.Bacc("TRN2", target_bir_lowering=False, num_devices=1)
    arrays, args = {}, []
    for name in _INS:
        a = _np.ascontiguousarray(inputs[name])
        arrays[f"in_{name}"] = a
        args.append(nc.dram_tensor(f"in_{name}", a.shape, _mybir.dt.from_np(a.dtype), kind="ExternalInput").ap())
    shape = arrays["in_x"].shape
    args.append(nc.dram_tensor("out_0", shape, _mybir.dt.float32, kind="ExternalOutput").ap())
    xattn_block(nc, *args)
    r = _run(nc, [arrays], core_ids=[0])
    return r.results[0]["out_0"]
```

```python
import concourse.bass as bass
from concourse import mybir
from contextlib import ExitStack


def xattn_block(nc, x, ctx, mask, qn_w, qn_b, cn_w, cn_b, n2_w, n2_b, q_w, kv_w, proj_w, proj_b,
                fc1_w, fc1_b, fc2_w, fc2_b, out):
    F32 = mybir.dt.float32
    F32R = mybir.dt.float32r
    BF16 = mybir.dt.bfloat16
    ALU = mybir.AluOpType
    ACT = mybir.ActivationFunctionType
    X = mybir.AxisListType.X

    B, N, C = x.shape
    M = ctx.shape[1]
    HID = fc1_w.shape[1]
    H, D = 16, 16
    P = 128
    EPS = 1e-5
    SCALE = float(D) ** -0.5
    MASKED = -float(2 ** 127)
    NB = 2
    PAIRS = B // NB
    TT = NB * N // P
    KC = C // P
    HC = HID // P
    G = H * D // P
    HG = H // G
    UNITS = TT * G
    BG = NB * G
    MP = -(-M // D) * D
    NM = HG * MP // P
    HM = HG // 2 * M
    TN = TT * P
    HALF = P // 2
    K_STEPS = G + 4 + 2

    es = ExitStack()
    with es:
        def sb(name, shape, dt=F32):
            return es.enter_context(nc.sbuf_tensor(name, shape, dt))

        def sem(name):
            return es.enter_context(nc.semaphore(name))

        qw_hi, qw_lo = sb("qw_hi", [P, KC, C], F32R), sb("qw_lo", [P, KC, C], F32R)
        kvw_hi, kvw_lo = sb("kvw_hi", [P, KC, 2 * C], F32R), sb("kvw_lo", [P, KC, 2 * C], F32R)
        pw_hi, pw_lo = sb("pw_hi", [P, KC, C], F32R), sb("pw_lo", [P, KC, C], F32R)
        w1_hi, w1_lo = sb("w1_hi", [P, KC, HID], F32R), sb("w1_lo", [P, KC, HID], F32R)
        w2_hi, w2_lo = sb("w2_hi", [P, HC, C], F32R), sb("w2_lo", [P, HC, C], F32R)
        vec_rows = sb("vec_rows", [6 * KC + HC, P])
        vecs = sb("vecs", [P, 6, KC])
        fc1b = sb("fc1b", [P, HC])
        bias = sb("bias", [P, 2 * G + HC])
        bv = sb("bv", [M, C])
        projb = sb("projb", [P, C])
        fc2b = sb("fc2b", [P, C])
        ident = sb("ident", [P, P])
        ident_bf = sb("ident_bf", [P, P], BF16)
        head_of = sb("head_of", [P, HG])
        head_of4 = sb("head_of4", [P, HG // 2])
        chunk_head = sb("chunk_head", [P, NM, HG])
        neg_half = sb("neg_half", [P, TT + NB])
        eps = sb("eps", [P, TT + NB])
        NP = 4
        probs = [sb(f"probs{u}", [P, HG, MP]) for u in range(NP)]
        flat = [p[:].rearrange("p h m -> p (h m)") for p in probs]
        probsT = [sb(f"probsT{k}", [P, NM, N]) for k in range(2)]
        g_f = [sb(f"g_f{k}", [P, TN]) for k in range(2)]

        xin = [sb(f"xin{k}", [P, TT, C]) for k in range(2)]
        x1 = [sb(f"x1_{k}", [P, TT, C]) for k in range(2)]
        ctxin = sb("ctxin", [M, NB, C])
        xn = sb("xn", [P, TT, C])
        cn = sb("cn", [M, NB, C])
        stats = sb("stats", [P, TT + NB, 6])
        moms = sb("moms", [P, TT + NB, 2])
        rstd = sb("rstd", [P, TT + NB])
        stats2 = sb("stats2", [P, TT, 6])
        moms2 = sb("moms2", [P, TT, 2])
        rstd2 = sb("rstd2", [P, TT])
        hn = xn
        xT_hi, xT_lo = sb("xT_hi", [P, KC, TN], F32R), sb("xT_lo", [P, KC, TN], F32R)
        hT_hi, hT_lo = sb("hT_hi", [P, KC, TN], F32R), sb("hT_lo", [P, KC, TN], F32R)
        cT_hi, cT_lo = sb("cT_hi", [P, KC, NB * M], F32R), sb("cT_lo", [P, KC, NB * M], F32R)
        q_st = sb("q_st", [P, G, 2, TN], F32R)
        k_st = sb("k_st", [P, 2, G, NB, M])
        k_lo = sb("k_lo", [P, G, NB, M])
        kd_st = sb("kd_st", [P, BG, 2, HM], F32R)
        kd_lo = sb("kd_lo", [P, BG, HM], F32R)
        v_rows = sb("v_rows", [MP, NB * C])
        v_rep = sb("v_rep", [P, BG, NM, D])
        vd = sb("vd", [P, BG, NM, HG * D])
        mask_u8 = sb("mask_u8", [P, TT, M], mask.dtype)
        mask_b = [sb(f"mask_b{k}", [P, TT, M], BF16) for k in range(2)]
        rmax = [sb(f"rmax{k}", [P, HG]) for k in range(2)]
        carrier = sb("carrier", [P, 1])
        rsum = sb("rsum", [P, HG])
        rinv = [sb(f"rinv{k}", [P, HG]) for k in range(NP)]
        oT_hi, oT_lo = sb("oT_hi", [P, G, TN], F32R), sb("oT_lo", [P, G, TN], F32R)
        with ExitStack() as first_user:
            def raw(name, k, n):
                return first_user.enter_context(nc.sbuf_tensor(name, [P, k, n], F32))
            raw_w1, raw_w2 = raw("raw_w1", KC, HID), raw("raw_w2", HC, C)
            raw_q, raw_kv, raw_p = raw("raw_q", KC, C), raw("raw_kv", KC, 2 * C), raw("raw_p", KC, C)
        g_hi, g_lo = sb("g_hi", [P, HC, TN], F32R), sb("g_lo", [P, HC, TN], F32R)

        v_dram = nc.dram_tensor("v_dram", [2, NB * H, MP, D], F32, kind="Internal").ap()

        S = es.enter_context(nc.psum_tensor("S", [P, 2, 512], F32))
        T = [es.enter_context(nc.psum_tensor(f"T{k}", [P, 512], F32)) for k in range(2)]
        R = es.enter_context(nc.psum_tensor("R", [P, 512], F32))
        ctx_cols = R[:, 0:KC * NB * M].rearrange("p (k n) -> p k n", k=KC)
        Q = es.enter_context(nc.psum_tensor("Q", [P, 512], F32))
        F = [es.enter_context(nc.psum_tensor(f"F{k}", [P, 512], F32)) for k in range(2)]

        consts = sem("consts")
        qkv_loaded = sem("qkv_loaded")
        pw_loaded = sem("pw_loaded")
        mlp_loaded = sem("mlp_loaded")
        vecs_loaded = sem("vecs_loaded")
        rows_loaded = sem("rows_loaded")
        vecs_mm = sem("vecs_mm")
        vecs_done = sem("vecs_done")
        bias_mm = sem("bias_mm")
        w_hi_done = sem("w_hi_done")
        setup_done = sem("setup_done")
        x_loaded = sem("x_loaded")
        ctx_loaded = sem("ctx_loaded")
        mask_loaded = sem("mask_loaded")
        mask_ready = sem("mask_ready")
        stats_done = sem("stats_done")
        moms_done = sem("moms_done")
        rstd_step = sem("rstd_step")
        xn_done = sem("xn_done")
        cn_done = sem("cn_done")
        xb_done = sem("xb_done")
        cT_mm = sem("cT_mm")
        cT_hi_done = sem("cT_hi_done")
        cT_lo_done = sem("cT_lo_done")
        xT_mm = sem("xT_mm")
        xT_hi_done = sem("xT_hi_done")
        xT_lo_done = sem("xT_lo_done")
        k_mm = sem("k_mm")
        k_step = sem("k_step")
        kd_done = sem("kd_done")
        v_mm = sem("v_mm")
        v_rows_done = sem("v_rows_done")
        v_stored = sem("v_stored")
        v_gathered = sem("v_gathered")
        vd_done = sem("vd_done")
        q_mm = sem("q_mm")
        q_hi_done = sem("q_hi_done")
        q_lo_done = sem("q_lo_done")
        s_mm = sem("s_mm")
        max_done = sem("max_done")
        shifted = sem("shifted")
        exp_done = sem("exp_done")
        sum_done = sem("sum_done")
        rinv_done = sem("rinv_done")
        weighed = sem("weighed")
        pT_mm = sem("pT_mm")
        pT_done = sem("pT_done")
        o_mm = sem("o_mm")
        o_hi_done = sem("o_hi_done")
        o_lo_done = sem("o_lo_done")
        proj_mm = sem("proj_mm")
        x1_done = sem("x1_done")
        stats2_done = sem("stats2_done")
        moms2_done = sem("moms2_done")
        rstd2_step = sem("rstd2_step")
        hn_done = sem("hn_done")
        x1b_done = sem("x1b_done")
        hT_mm = sem("hT_mm")
        hT_hi_done = sem("hT_hi_done")
        hT_lo_done = sem("hT_lo_done")
        f1_mm = sem("f1_mm")
        gelu_done = sem("gelu_done")
        g_hi_done = sem("g_hi_done")
        g_lo_done = sem("g_lo_done")
        f2_mm = sem("f2_mm")
        y_done = sem("y_done")
        y_stored = sem("y_stored")

        def least(n):
            return max(n, 0) if isinstance(n, int) else n

        def mlp_weight_part(n):
            if n < 4:
                k, cols = n // 2, slice(n % 2 * (HID // 2), (n % 2 + 1) * (HID // 2))
                return w1_hi[:, k, cols], w1_lo[:, k, cols], raw_w1[:, k, cols], k
            k = slice(n % 4 * (HC // 4), (n % 4 + 1) * (HC // 4))
            return w2_hi[:, k], w2_lo[:, k], raw_w2[:, k], None

        def min_pair(j):
            return min(j, PAIRS) if isinstance(j, int) else j

        def pairs_of(eng, body):
            body(0, 0, False, True, True)
            body(1, 1, True, True, True)
            with eng.Fori(0, PAIRS // 2 - 2) as i:
                body(2 * i + 2, 0, True, True, True)
                body(2 * i + 3, 1, True, True, True)
            body(PAIRS - 2, 0, True, True, False)
            body(PAIRS - 1, 1, True, False, False)

        block = es.enter_context(nc.Block())

        @block.sync
        def _(sp):
            def load_x(j, par):
                if not isinstance(j, int):
                    sp.wait_ge(consts, CONSTS)
                sp.wait_ge(x1_done, least(2 * (j - 1)))
                sp.dma_start(xin[par][:], x.rearrange("b (t p) c -> p (b t) c", p=P)[:, bass.ts(j, TT), :]).then_inc(x_loaded, 16)

            def load_ctx(j):
                if not isinstance(j, int):
                    sp.wait_ge(consts, CONSTS)
                sp.wait_ge(cn_done, NB * j)
                sp.dma_start(ctxin[:], ctx.rearrange("b m c -> m b c")[:, bass.ts(j, NB), :]).then_inc(ctx_loaded, 16)

            def load_mask(j):
                if not isinstance(j, int):
                    sp.wait_ge(consts, CONSTS)
                sp.wait_ge(mask_ready, j)
                sp.dma_start(mask_u8[:], mask.rearrange("b (t p) m -> p (b t) m", p=P)[:, bass.ts(j, TT), :]).then_inc(mask_loaded, 16)

            def spread_v(j, par):
                sp.wait_ge(v_rows_done, j + 1)
                sp.dma_start(v_dram[par].rearrange("x m d -> m x d"), v_rows[:].rearrange("m (x d) -> m x d", d=D)).then_inc(v_stored, 16)
                sp.wait_ge(v_stored, 16 * (j + 1))
                sp.wait_ge(vd_done, BG * j)
                sp.dma_start(v_rep[:], v_dram[par].rearrange("(g h) m d -> g (h m) d", h=HG)
                             .rearrange("g (c p) d -> p g c d", p=P)).then_inc(v_gathered, 16)

            def store(j, par, half):
                sp.wait_ge(consts, CONSTS)
                sp.wait_ge(y_done, 2 * j + half + 1)
                dst = out.rearrange("b (t p) c -> p (b t) c", p=P)
                sp.dma_start(dst[:, bass.ds(j * TT + half * 2, 2), :], x1[par][:, 2 * half:2 * half + 2]).then_inc(y_stored, 16)

            load_ctx(0)
            load_x(0, 0)
            for dst, src in ((raw_kv, kv_w), (raw_q, q_w)):
                sp.dma_start(dst[:], src.rearrange("(k p) n -> p k n", p=P)).then_inc(qkv_loaded, 16)
            load_mask(0)
            sp.wait_ge(vecs_loaded, 7 * 16)
            sp.wait_ge(qkv_loaded, 2 * 16)
            sp.dma_start(raw_p[:], proj_w.rearrange("(k p) n -> p k n", p=P)).then_inc(pw_loaded, 16)
            for dst, src in ((raw_w1, fc1_w), (raw_w2, fc2_w)):
                sp.dma_start(dst[:], src.rearrange("(k p) n -> p k n", p=P)).then_inc(mlp_loaded, 16)
            load_ctx(1)
            spread_v(0, 0)
            load_mask(1)

            def body(j, par, mlp, prep, ahead):
                if prep:
                    load_x(j + 1, 1 - par)
                if ahead:
                    load_ctx(j + 2)
                if prep:
                    spread_v(j + 1, 1 - par)
                if ahead:
                    load_mask(j + 2)
                if mlp:
                    store(j - 1, 1 - par, 0)
                    store(j - 1, 1 - par, 1)
            pairs_of(sp, body)
            store(PAIRS - 1, 1, 0)
            store(PAIRS - 1, 1, 1)
            sp.wait_ge(y_stored, 32 * PAIRS)
            sp.wait_ge(v_stored, 16 * PAIRS)

        @block.gpsimd
        def _(pool):
            pool.memset(ident[:], 0.0).then_inc(consts, 1)
            pool.memset(head_of[:], 1.0).then_inc(consts, 1)
            pool.memset(chunk_head[:], 1.0).then_inc(consts, 1)
            pool.memset(neg_half[:], -0.5).then_inc(consts, 1)
            pool.memset(eps[:], EPS).then_inc(consts, 1)
            pool.memset(v_rows[:], 0.0).then_inc(consts, 1)
            pool.memset(moms[:], 1.0).then_inc(consts, 1)
            pool.wait_ge(consts, 7)
            pool.affine_select(out=ident[:], in_=ident[:], compare_op=ALU.not_equal, fill=1.0, base=0,
                               pattern=[[-1, P]], channel_multiplier=1).then_inc(consts, 1)
            pool.affine_select(out=head_of[:], in_=head_of[:], compare_op=ALU.is_ge, fill=0.0, base=0,
                               pattern=[[-D, HG]], channel_multiplier=1).then_inc(consts, 1)
            pool.affine_select(out=chunk_head[:], in_=chunk_head[:], compare_op=ALU.is_ge, fill=0.0, base=0,
                               pattern=[[P, NM], [-MP, HG]], channel_multiplier=1).then_inc(consts, 1)
            pool.wait_ge(consts, 10)
            pool.affine_select(out=head_of[:], in_=head_of[:], compare_op=ALU.is_ge, fill=0.0, base=D - 1,
                               pattern=[[D, HG]], channel_multiplier=-1).then_inc(consts, 1)
            pool.affine_select(out=chunk_head[:], in_=chunk_head[:], compare_op=ALU.is_ge, fill=0.0, base=MP - 1,
                               pattern=[[-P, NM], [MP, HG]], channel_multiplier=-1).then_inc(consts, 1)
            pool.wait_ge(consts, 12)
            pool.tensor_tensor(head_of4[:], head_of[:, 0:HG // 2], head_of[:, HG // 2:], ALU.add).then_inc(consts, 1)
            pool.wait_ge(consts, CONSTS)

            def rstd_x(j):
                pool.wait_ge(xn_done, TT * j)
                pool.wait_ge(cn_done, NB * j)
                pool.wait_ge(moms_done, (TT + NB) * (j + 1))
                pool.tensor_tensor(rstd[:], moms[:, :, 1], eps[:], ALU.add).then_inc(rstd_step, 1)
                pool.wait_ge(rstd_step, 2 * j + 1)
                pool.tensor_tensor(rstd[:], rstd[:], neg_half[:], ALU.pow).then_inc(rstd_step, 1)

            def rstd_h(j):
                pool.wait_ge(hn_done, TT * j)
                pool.wait_ge(moms2_done, TT * (j + 1))
                pool.tensor_tensor(rstd2[:], moms2[:, :, 1], eps[:, 0:TT], ALU.add).then_inc(rstd2_step, 1)
                pool.wait_ge(rstd2_step, 2 * j + 1)
                pool.tensor_tensor(rstd2[:], rstd2[:], neg_half[:, 0:TT], ALU.pow).then_inc(rstd2_step, 1)

            def add_proj_b(j, par):
                pool.wait_ge(xn_done, TT * (j + 1))
                pool.tensor_tensor(xin[par][:], xin[par][:], projb[:].unsqueeze(1).to_broadcast([P, TT, C]),
                                   ALU.add).then_inc(xb_done, 1)

            def add_fc2_b(j, par):
                pool.wait_ge(hn_done, TT * (j + 1))
                pool.tensor_tensor(x1[par][:], x1[par][:], fc2b[:].unsqueeze(1).to_broadcast([P, TT, C]),
                                   ALU.add).then_inc(x1b_done, 1)

            def spread_k(j, bg):
                b, g = divmod(bg, G)
                pool.wait_ge(k_step, K_STEPS * (j + 1))
                pool.wait_ge(s_mm, least(UNITS * (j - 1) + 2 * bg + 2))
                for part, src in ((kd_st[:, bg, 0], k_st[:, 0, g, b]), (kd_st[:, bg, 1], k_st[:, 1, g, b]),
                                  (kd_lo[:, bg], k_lo[:, g, b])):
                    pool.tensor_tensor(part.rearrange("p (h m) -> p h m", m=M),
                                       src.unsqueeze(1).to_broadcast([P, HG // 2, M]),
                                       head_of4[:].unsqueeze(2).to_broadcast([P, HG // 2, M]), ALU.mult).then_inc(kd_done, 1)

            def spread_v(j, bg):
                pool.wait_ge(v_gathered, 16 * (j + 1))
                pool.wait_ge(o_mm, least(BG * (j - 1) + bg + 1))
                pool.tensor_tensor(vd[:, bg].rearrange("p c (h d) -> p c h d", d=D),
                                   v_rep[:, bg].unsqueeze(2).to_broadcast([P, NM, HG, D]),
                                   chunk_head[:].unsqueeze(3).to_broadcast([P, NM, HG, D]),
                                   ALU.mult).then_inc(vd_done, 1)

            def weigh(j, u):
                pool.wait_ge(rinv_done, UNITS * j + u + 1)
                p = probs[u % NP][:, :, 0:M]
                pool.tensor_tensor(p, p, rinv[u % NP][:].unsqueeze(2).to_broadcast([P, HG, M]),
                                   ALU.mult).then_inc(weighed, 1)

            rstd_x(0)
            pool.wait_ge(rows_loaded, 2 * 16)
            add_proj_b(0, 0)
            for bg in range(BG):
                spread_k(0, bg)
            for bg in range(BG):
                spread_v(0, bg)
            weigh(0, 0)
            weigh(0, 1)
            weigh(0, 2)

            def body(j, par, mlp, prep, ahead):
                weigh(j, 3)
                if prep:
                    rstd_x(j + 1)
                weigh(j, 4)
                weigh(j, 5)
                if prep:
                    add_proj_b(j + 1, 1 - par)
                if mlp:
                    add_fc2_b(j - 1, 1 - par)
                weigh(j, 6)
                if prep:
                    spread_k(j + 1, 0)
                    spread_v(j + 1, 0)
                weigh(j, 7)
                if prep:
                    spread_v(j + 1, 1)
                    spread_k(j + 1, 1)
                    spread_v(j + 1, 2)
                    spread_k(j + 1, 2)
                    weigh(j + 1, 0)
                    weigh(j + 1, 1)
                    spread_k(j + 1, 3)
                    spread_v(j + 1, 3)
                    weigh(j + 1, 2)
                rstd_h(j)
            pairs_of(pool, body)
            add_fc2_b(PAIRS - 1, 1)

        @block.scalar
        def _(act):
            for k, v in enumerate((qn_w, qn_b, cn_w, cn_b, n2_w, n2_b)):
                act.dma_start(vec_rows[k * KC:(k + 1) * KC], v.rearrange("(k p) -> k p", p=P)).then_inc(vecs_loaded, 16)
            act.dma_start(vec_rows[6 * KC:], fc1_b.rearrange("(k p) -> k p", p=P)).then_inc(vecs_loaded, 16)
            act.dma_start(projb[:], proj_b.unsqueeze(0).to_broadcast([P, C])).then_inc(rows_loaded, 16)
            act.dma_start(fc2b[:], fc2_b.unsqueeze(0).to_broadcast([P, C])).then_inc(rows_loaded, 16)
            act.wait_ge(vecs_done, 2)
            act.wait_ge(qkv_loaded, 2 * 16)
            for hi, raw, nw in ((kvw_hi, raw_kv, 2), (qw_hi, raw_q, 0)):
                for k in range(KC):
                    act.activation(hi[:, k], raw[:, k], ACT.Copy, scale=vecs[:, nw, k:k + 1]).then_inc(w_hi_done, 1)

            def proj_weight_high():
                act.wait_ge(pw_loaded, 16)
                act.activation(pw_hi[:], raw_p[:], ACT.Copy).then_inc(w_hi_done, 1)

            def mlp_weight_high(n):
                act.wait_ge(mlp_loaded, 2 * 16)
                hi, _, raw, k = mlp_weight_part(n)
                if n < 4:
                    act.activation(hi, raw, ACT.Copy, scale=vecs[:, 4, k:k + 1]).then_inc(w_hi_done, 1)
                else:
                    act.activation(hi, raw, ACT.Copy).then_inc(w_hi_done, 1)

            def cT_high(j):
                act.wait_ge(cT_mm, j + 1)
                act.wait_ge(k_mm, j)
                act.wait_ge(v_mm, j)
                act.activation(cT_hi[:], ctx_cols, ACT.Copy).then_inc(cT_hi_done, 1)

            def xT_high(j, k):
                act.wait_ge(xT_mm, KC * j + k + 1)
                act.wait_ge(q_mm, G * j)
                act.activation(xT_hi[:, k], R[:], ACT.Copy).then_inc(xT_hi_done, 1)

            def q_high(j, g):
                act.wait_ge(q_mm, G * j + g + 1)
                act.wait_ge(s_mm, least(UNITS * (j - 1) + 6 + 2 * g))
                for a in range(2):
                    rows = slice(a * HALF, (a + 1) * HALF)
                    act.activation(q_st[rows, g, a], Q[rows, :], ACT.Identity, bias=bias[rows, g:g + 1]).then_inc(q_hi_done, 1)

            def exp(j, u):
                act.wait_ge(shifted, UNITS * j + u + 1)
                act.activation(probs[u % NP][:, :, 0:M], probs[u % NP][:, :, 0:M], ACT.Exp, scale=SCALE).then_inc(exp_done, 1)

            def pT_copy(j, bg, s):
                n = 1 if s == 2 else 2
                act.wait_ge(pT_mm, 3 * (BG * j + bg) + s + 1)
                act.wait_ge(o_mm, least(BG * j + bg - 1))
                act.activation(probsT[bg % 2][:, 2 * s:2 * s + n], T[(3 * bg + s) % 2][:, 0:n * N].rearrange("p (c n) -> p c n", n=N),
                               ACT.Copy).then_inc(pT_done, 1)

            def high_o(j, bg):
                b, g = divmod(bg, G)
                act.wait_ge(o_mm, BG * j + bg + 1)
                act.wait_ge(proj_mm, least(2 * (j - 1) + b + 1))
                act.activation(oT_hi[:, g, b * N:(b + 1) * N], Q[:, 0:N], ACT.Copy).then_inc(o_hi_done, 1)

            def hT_high(j, k):
                act.wait_ge(setup_done, ALL_READY)
                act.wait_ge(hT_mm, KC * j + k + 1)
                act.wait_ge(f1_mm, HC * j)
                act.activation(hT_hi[:, k], F[k][:], ACT.Copy).then_inc(hT_hi_done, 1)

            def gelu(j, k):
                act.wait_ge(f1_mm, HC * j + k + 1)
                act.wait_ge(g_lo_done, least(HC * j + max(k - 1, 0)))
                act.wait_ge(f2_mm, 2 * j)
                b1 = bias[:, 2 * G + k:2 * G + k + 1]
                act.activation(g_f[k % 2][:], F[k % 2][:], ACT.Gelu, bias=b1).then_inc(gelu_done, 1)
                act.activation(g_hi[:, k], F[k % 2][:], ACT.Gelu, bias=b1).then_inc(g_hi_done, 1)

            cT_high(0)
            xT_high(0, 0)
            xT_high(0, 1)
            act.wait_ge(setup_done, QKV_READY)
            q_high(0, 0)
            q_high(0, 1)
            exp(0, 0)
            exp(0, 1)
            exp(0, 2)
            exp(0, 3)
            pT_copy(0, 0, 0)

            def body(j, par, mlp, prep, ahead):
                pT_copy(j, 0, 1)
                pT_copy(j, 0, 2)
                pT_copy(j, 1, 0)
                if mlp:
                    hT_high(j - 1, 0)
                else:
                    proj_weight_high()
                if mlp:
                    hT_high(j - 1, 1)
                exp(j, 4)
                pT_copy(j, 1, 1)
                high_o(j, 0)
                if mlp:
                    gelu(j - 1, 0)
                else:
                    mlp_weight_high(0)
                pT_copy(j, 1, 2)
                if mlp:
                    gelu(j - 1, 1)
                else:
                    mlp_weight_high(1)
                exp(j, 5)
                if prep:
                    cT_high(j + 1)
                high_o(j, 1)
                exp(j, 6)
                if mlp:
                    gelu(j - 1, 2)
                else:
                    mlp_weight_high(2)
                if prep:
                    xT_high(j + 1, 0)
                if mlp:
                    gelu(j - 1, 3)
                else:
                    mlp_weight_high(3)
                if prep:
                    xT_high(j + 1, 1)
                if mlp:
                    gelu(j - 1, 4)
                else:
                    mlp_weight_high(4)
                pT_copy(j, 2, 0)
                if mlp:
                    gelu(j - 1, 5)
                else:
                    mlp_weight_high(5)
                if prep:
                    q_high(j + 1, 0)
                pT_copy(j, 2, 1)
                if mlp:
                    gelu(j - 1, 6)
                else:
                    mlp_weight_high(6)
                if mlp:
                    gelu(j - 1, 7)
                else:
                    mlp_weight_high(7)
                exp(j, 7)
                if prep:
                    q_high(j + 1, 1)
                pT_copy(j, 2, 2)
                if prep:
                    exp(j + 1, 0)
                pT_copy(j, 3, 0)
                pT_copy(j, 3, 1)
                if prep:
                    exp(j + 1, 1)
                high_o(j, 2)
                pT_copy(j, 3, 2)
                high_o(j, 3)
                if prep:
                    exp(j + 1, 2)
                    exp(j + 1, 3)
                    pT_copy(j + 1, 0, 0)
            pairs_of(act, body)
            hT_high(PAIRS - 1, 0)
            hT_high(PAIRS - 1, 1)
            for k in range(HC):
                gelu(PAIRS - 1, k)

        @block.vector
        def _(dve):
            def low(dst, src, hi):
                return dve.tensor_tensor(dst, src, hi.bitcast(F32), ALU.subtract)

            def ln_stats(j, par):
                dve.wait_ge(rstd_step, 2 * j)
                dve.wait_ge(x_loaded, 16 * (j + 1))
                for t in range(TT):
                    dve.bn_stats(stats[:, t], xin[par][:, t]).then_inc(stats_done, 1)
                dve.wait_ge(ctx_loaded, 16 * (j + 1))
                for b in range(NB):
                    dve.bn_stats(stats[0:M, TT + b], ctxin[:, b]).then_inc(stats_done, 1)

            def ln_moments(j):
                dve.wait_ge(stats_done, (TT + NB) * (j + 1))
                dve.memset(carrier[:], 0.0)
                for t in range(TT):
                    dve.bn_aggr(moms[:, t], stats[:, t]).then_inc(moms_done, 1)
                for b in range(NB):
                    dve.bn_aggr(moms[0:M, TT + b], stats[0:M, TT + b]).then_inc(moms_done, 1)

            def normalise_ctx(j):
                dve.wait_ge(rstd_step, 2 * (j + 1))
                dve.wait_ge(cT_mm, j)
                for b in range(NB):
                    dve.tensor_scalar(cn[:, b], ctxin[:, b], moms[0:M, TT + b, 0:1], rstd[0:M, TT + b:TT + b + 1],
                                      ALU.subtract, ALU.mult).then_inc(cn_done, 1)

            def normalise_x(j, par):
                dve.wait_ge(rstd_step, 2 * (j + 1))
                dve.wait_ge(hT_mm, least(KC * (j - 1)))
                for t in range(TT):
                    dve.tensor_scalar(xn[:, t], xin[par][:, t], moms[:, t, 0:1], rstd[:, t:t + 1],
                                      ALU.subtract, ALU.mult).then_inc(xn_done, 1)

            def mask_bias(j, par):
                dve.wait_ge(mask_loaded, 16 * (j + 1))
                dve.wait_ge(s_mm, least(UNITS * (j - 1)))
                dve.tensor_scalar(mask_b[par][:], mask_u8[:], MASKED, None, ALU.mult).then_inc(mask_ready, 1)

            def cT_low(j):
                dve.wait_ge(cT_hi_done, j + 1)
                low(cT_lo[:], ctx_cols, cT_hi[:]).then_inc(cT_lo_done, 1)

            def xT_low(j, k):
                dve.wait_ge(xT_hi_done, KC * j + k + 1)
                low(xT_lo[:, k], R[:], xT_hi[:, k]).then_inc(xT_lo_done, 1)

            def k_evacuate(j):
                dve.wait_ge(k_mm, j + 1)
                dve.wait_ge(kd_done, 3 * BG * j)
                for g in range(G):
                    dve.tensor_scalar(k_lo[:, g].rearrange("p b m -> p (b m)"), ctx_cols[:, g],
                                      bias[:, G + g:G + g + 1], None, ALU.add).then_inc(k_step, 1)

            def k_split(j):
                dve.wait_ge(k_step, K_STEPS * j + G)
                for a in range(2):
                    rows, other = slice(a * HALF, (a + 1) * HALF), slice((1 - a) * HALF, (2 - a) * HALF)
                    dve.tensor_copy(k_st[rows, a].bitcast(F32R), k_lo[rows]).then_inc(k_step, 1)
                    dve.tensor_copy(k_st[other, a].bitcast(F32R), k_lo[rows]).then_inc(k_step, 1)
                dve.wait_ge(k_step, K_STEPS * j + G + 4)
                for a in range(2):
                    rows = slice(a * HALF, (a + 1) * HALF)
                    dve.tensor_tensor(k_lo[rows], k_lo[rows], k_st[rows, a], ALU.subtract).then_inc(k_step, 1)

            def v_evacuate(j):
                dve.wait_ge(v_mm, j + 1)
                dve.wait_ge(v_stored, 16 * j)
                dve.tensor_tensor(v_rows[0:M].rearrange("p (b c) -> p b c", c=C), Q[0:M, :].rearrange("p (b c) -> p b c", c=C),
                                  bv[:].unsqueeze(1).to_broadcast([M, NB, C]), ALU.add).then_inc(v_rows_done, 1)

            def q_low(j, g):
                dve.wait_ge(q_hi_done, 2 * (G * j + g + 1))
                for a in range(2):
                    rows, other = slice(a * HALF, (a + 1) * HALF), slice((1 - a) * HALF, (2 - a) * HALF)
                    dve.scalar_tensor_tensor(out=q_st[other, g, a], in0=Q[rows, :], scalar=bias[rows, g:g + 1],
                                             in1=q_st[rows, g, a].bitcast(F32), op0=ALU.add, op1=ALU.subtract).then_inc(q_lo_done, 1)

            def unit_views(u):
                return (S[:, :, 0:HM].rearrange("p a (h m) -> p a h m", m=M),
                        rmax[u % 2][:].rearrange("p (a h) -> p a h", a=2))

            def row_max(j, u):
                sc, mx = unit_views(u)
                dve.wait_ge(s_mm, UNITS * j + u + 1)
                dve.wait_ge(shifted, least(UNITS * j + u - 1))
                dve.tensor_reduce(mx, sc, X, ALU.max).then_inc(max_done, 1)

            def shift(j, u):
                sc, mx = unit_views(u)
                dve.wait_ge(max_done, UNITS * j + u + 1)
                dve.wait_ge(pT_mm, least(3 * (BG * j + (u - NP) // 2 + 1)))
                dve.tensor_tensor(probs[u % NP][:, :, 0:M].rearrange("p (a h) m -> p a h m", a=2), sc,
                                  mx.unsqueeze(3).to_broadcast([P, 2, HG // 2, M]), ALU.subtract).then_inc(shifted, 1)

            def row_sum(j, u):
                dve.wait_ge(exp_done, UNITS * j + u + 1)
                dve.wait_ge(rinv_done, UNITS * j + u)
                dve.tensor_reduce(rsum[:], probs[u % NP][:, :, 0:M], X, ALU.add).then_inc(sum_done, 1)
                dve.wait_ge(sum_done, UNITS * j + u + 1)
                dve.wait_ge(weighed, least(UNITS * j + u - NP + 1))
                dve.reciprocal(rinv[u % NP][:], rsum[:]).then_inc(rinv_done, 1)

            def low_o(j, bg):
                b, g = divmod(bg, G)
                cols = slice(b * N, (b + 1) * N)
                dve.wait_ge(o_hi_done, BG * j + bg + 1)
                low(oT_lo[:, g, cols], Q[:, 0:N], oT_hi[:, g, cols]).then_inc(o_lo_done, 1)

            def add_x(j, par, half):
                dve.wait_ge(proj_mm, 2 * j + half + 1)
                dve.wait_ge(xb_done, j + 1)
                dve.wait_ge(y_stored, least(32 * (j - 1)))
                dve.tensor_tensor(x1[par][:, 2 * half:2 * half + 2], Q[:].rearrange("p (t c) -> p t c", c=C),
                                  xin[par][:, 2 * half:2 * half + 2], ALU.add).then_inc(x1_done, 1)

            def h_stats(j, par, half):
                dve.wait_ge(x1_done, 2 * j + half + 1)
                dve.wait_ge(rstd2_step, 2 * j)
                for t in (2 * half, 2 * half + 1):
                    dve.bn_stats(stats2[:, t], x1[par][:, t]).then_inc(stats2_done, 1)

            def h_moments(j):
                dve.wait_ge(stats2_done, TT * (j + 1))
                dve.memset(carrier[:], 0.0)
                for t in range(TT):
                    dve.bn_aggr(moms2[:, t], stats2[:, t]).then_inc(moms2_done, 1)

            def h_normalise(j, par):
                dve.wait_ge(rstd2_step, 2 * (j + 1))
                dve.wait_ge(xT_mm, KC * min_pair(j + 2))
                for t in range(TT):
                    dve.tensor_scalar(hn[:, t], x1[par][:, t], moms2[:, t, 0:1], rstd2[:, t:t + 1],
                                      ALU.subtract, ALU.mult).then_inc(hn_done, 1)

            def hT_low(j, k):
                dve.wait_ge(hT_hi_done, KC * j + k + 1)
                low(hT_lo[:, k], F[k][:], hT_hi[:, k]).then_inc(hT_lo_done, 1)

            def g_low(j, k):
                dve.wait_ge(gelu_done, HC * j + k + 1)
                dve.wait_ge(g_hi_done, HC * j + k + 1)
                low(g_lo[:, k], g_f[k % 2][:], g_hi[:, k]).then_inc(g_lo_done, 1)

            def add_x1(j, par, half):
                dve.wait_ge(f2_mm, 2 * j + half + 1)
                dve.wait_ge(x1b_done, j + 1)
                dve.tensor_tensor(x1[par][:, 2 * half:2 * half + 2], F[half][:].rearrange("p (t c) -> p t c", c=C),
                                  x1[par][:, 2 * half:2 * half + 2], ALU.add).then_inc(y_done, 1)

            def weight_low(lo, raw, hi, nw, k, n):
                dve.wait_ge(w_hi_done, n)
                dve.scalar_tensor_tensor(out=lo, in0=raw, scalar=vecs[:, nw, k:k + 1], in1=hi.bitcast(F32),
                                         op0=ALU.mult, op1=ALU.subtract).then_inc(setup_done, 1)

            def proj_weight_low():
                dve.wait_ge(w_hi_done, 2 * KC + 1)
                low(pw_lo[:], raw_p[:], pw_hi[:]).then_inc(setup_done, 1)

            def mlp_weight_low(n):
                hi, lo, raw, k = mlp_weight_part(n)
                if n < 4:
                    weight_low(lo, raw, hi, 4, k, 2 * KC + 1 + n + 1)
                else:
                    dve.wait_ge(w_hi_done, 2 * KC + 1 + n + 1)
                    low(lo, raw, hi).then_inc(setup_done, 1)

            def fc1_bias_evacuate():
                dve.wait_ge(bias_mm, 3)
                dve.tensor_tensor(bias[:, 2 * G:], F[0][:, 2 * G:2 * G + HC], fc1b[:], ALU.add).then_inc(setup_done, 1)

            for u in range(NP):
                dve.memset(probs[u][:], 0.0).then_inc(setup_done, 1)
            dve.wait_ge(consts, CONSTS)
            dve.tensor_copy(ident_bf[:], ident[:]).then_inc(setup_done, 1)
            ln_stats(0, 0)
            ln_moments(0)
            dve.wait_ge(vecs_mm, 1)
            dve.tensor_copy(vecs[:].rearrange("p v k -> p (v k)"), F[1][:, 0:6 * KC]).then_inc(vecs_done, 1)
            dve.tensor_copy(fc1b[:], F[1][:, 6 * KC:6 * KC + HC]).then_inc(vecs_done, 1)
            normalise_ctx(0)
            normalise_x(0, 0)
            dve.wait_ge(vecs_done, 2)
            for k in range(KC):
                weight_low(kvw_lo[:, k], raw_kv[:, k], kvw_hi[:, k], 2, k, k + 1)
            cT_low(0)
            for k in range(KC):
                weight_low(qw_lo[:, k], raw_q[:, k], qw_hi[:, k], 0, k, KC + k + 1)
            xT_low(0, 0)
            dve.wait_ge(bias_mm, 2)
            dve.tensor_copy(bias[:, 0:2 * G], F[0][:, 0:2 * G]).then_inc(setup_done, 1)
            dve.tensor_copy(bv[:], F[1][0:M, 0:C]).then_inc(setup_done, 1)
            dve.wait_ge(setup_done, QKV_READY)
            k_evacuate(0)
            xT_low(0, 1)
            k_split(0)
            v_evacuate(0)
            q_low(0, 0)
            mask_bias(0, 0)
            q_low(0, 1)
            row_max(0, 0)
            shift(0, 0)
            row_sum(0, 0)
            row_max(0, 1)
            shift(0, 1)
            row_max(0, 2)
            shift(0, 2)
            row_sum(0, 1)
            row_max(0, 3)
            shift(0, 3)
            row_sum(0, 2)
            row_sum(0, 3)

            def body(j, par, mlp, prep, ahead):
                if mlp:
                    h_normalise(j - 1, 1 - par)
                row_max(j, 4)
                shift(j, 4)
                if mlp:
                    hT_low(j - 1, 0)
                else:
                    proj_weight_low()
                if mlp:
                    hT_low(j - 1, 1)
                if prep:
                    ln_stats(j + 1, 1 - par)
                    ln_moments(j + 1)
                row_max(j, 5)
                shift(j, 5)
                low_o(j, 0)
                if mlp:
                    g_low(j - 1, 0)
                else:
                    mlp_weight_low(0)
                if prep:
                    normalise_ctx(j + 1)
                row_max(j, 6)
                row_sum(j, 4)
                if prep:
                    mask_bias(j + 1, 1 - par)
                    normalise_x(j + 1, 1 - par)
                    cT_low(j + 1)
                shift(j, 6)
                low_o(j, 1)
                row_sum(j, 5)
                if prep:
                    k_evacuate(j + 1)
                if mlp:
                    g_low(j - 1, 1)
                else:
                    mlp_weight_low(1)
                add_x(j, par, 0)
                if mlp:
                    g_low(j - 1, 2)
                else:
                    mlp_weight_low(2)
                if prep:
                    xT_low(j + 1, 0)
                row_max(j, 7)
                if prep:
                    v_evacuate(j + 1)
                row_sum(j, 6)
                if mlp:
                    g_low(j - 1, 3)
                else:
                    mlp_weight_low(3)
                if prep:
                    xT_low(j + 1, 1)
                    k_split(j + 1)
                if mlp:
                    g_low(j - 1, 4)
                else:
                    mlp_weight_low(4)
                if mlp:
                    g_low(j - 1, 5)
                else:
                    mlp_weight_low(5)
                if prep:
                    q_low(j + 1, 0)
                shift(j, 7)
                if mlp:
                    g_low(j - 1, 6)
                else:
                    mlp_weight_low(6)
                if mlp:
                    g_low(j - 1, 7)
                else:
                    mlp_weight_low(7)
                if prep:
                    row_max(j + 1, 0)
                row_sum(j, 7)
                if prep:
                    shift(j + 1, 0)
                    row_sum(j + 1, 0)
                    q_low(j + 1, 1)
                    row_max(j + 1, 1)
                    shift(j + 1, 1)
                h_stats(j, par, 0)
                low_o(j, 2)
                if prep:
                    row_max(j + 1, 2)
                    shift(j + 1, 2)
                    row_sum(j + 1, 1)
                if mlp:
                    add_x1(j - 1, 1 - par, 0)
                else:
                    fc1_bias_evacuate()
                if prep:
                    row_max(j + 1, 3)
                low_o(j, 3)
                if prep:
                    shift(j + 1, 3)
                    row_sum(j + 1, 2)
                add_x(j, par, 1)
                h_stats(j, par, 1)
                h_moments(j)
                if prep:
                    row_sum(j + 1, 3)
                if mlp:
                    add_x1(j - 1, 1 - par, 1)
            pairs_of(dve, body)
            h_normalise(PAIRS - 1, 1)
            hT_low(PAIRS - 1, 0)
            hT_low(PAIRS - 1, 1)
            for k in range(HC):
                g_low(PAIRS - 1, k)
            add_x1(PAIRS - 1, 1, 0)
            add_x1(PAIRS - 1, 1, 1)

        @block.tensor
        def _(pe):
            def product(dst, terms, inc=None):
                n = 0
                for (a_hi, a_lo), (b_hi, b_lo) in terms:
                    for a, b in ((a_hi, b_hi), (a_hi, b_lo), (a_lo, b_hi)):
                        last = pe.matmul(dst, a, b, start=(n == 0), stop=(n == 3 * len(terms) - 1))
                        n += 1
                return last

            def cT(j):
                pe.wait_ge(cn_done, NB * (j + 1))
                for k in range(KC):
                    for b in range(NB):
                        last = pe.transpose(ctx_cols[:, k, b * M:(b + 1) * M], cn[:, b, k * P:(k + 1) * P], ident[0:M, 0:M])
                last.then_inc(cT_mm, 1)

            def xT(j, k):
                pe.wait_ge(xn_done, TT * (j + 1))
                for t in range(TT):
                    last = pe.transpose(R[:, t * P:(t + 1) * P], xn[:, t, k * P:(k + 1) * P], ident[:])
                last.then_inc(xT_mm, 1)

            def k_proj(j):
                pe.wait_ge(cT_lo_done, j + 1)
                for g in range(G):
                    cols = slice(g * P, (g + 1) * P)
                    last = product(ctx_cols[:, g],
                                   [((kvw_hi[:, k, cols], kvw_lo[:, k, cols]), (cT_hi[:, k], cT_lo[:, k])) for k in range(KC)])
                last.then_inc(k_mm, 1)

            def v_proj(j):
                pe.wait_ge(cT_lo_done, j + 1)
                for b in range(NB):
                    rows = slice(b * M, (b + 1) * M)
                    last = product(Q[0:M, b * C:(b + 1) * C],
                                   [((cT_hi[:, k, rows], cT_lo[:, k, rows]), (kvw_hi[:, k, C:], kvw_lo[:, k, C:])) for k in range(KC)])
                last.then_inc(v_mm, 1)

            def q_proj(j, g):
                pe.wait_ge(xT_lo_done, KC * (j + 1))
                cols = slice(g * P, (g + 1) * P)
                product(Q[:], [((qw_hi[:, k, cols], qw_lo[:, k, cols]), (xT_hi[:, k], xT_lo[:, k]))
                               for k in range(KC)]).then_inc(q_mm, 1)

            def scores(j, par, u):
                bg, t = divmod(u, 2)
                b, g = divmod(bg, G)
                tok = slice((2 * b + t) * P, (2 * b + t + 1) * P)
                pe.wait_ge(q_lo_done, 2 * (G * j + g + 1))
                pe.wait_ge(kd_done, 3 * (BG * j + bg + 1))
                pe.wait_ge(mask_ready, j + 1)
                pe.wait_ge(shifted, UNITS * j + u)
                for a in range(2):
                    dst = S[:, a, 0:HM]
                    rows = slice(a * HALF, (a + 1) * HALF)
                    pe.matmul(dst.rearrange("p (h m) -> p h m", m=M), ident_bf[:],
                              mask_b[par][:, 2 * b + t].unsqueeze(1).to_broadcast([P, HG // 2, M]), start=True, stop=False)
                    pe.matmul(dst, q_st[:, g, a, tok], kd_st[:, bg, a], start=False, stop=False)
                    last = pe.matmul(dst, q_st[rows, g, a, tok], kd_lo[rows, bg], start=False, stop=True)
                last.then_inc(s_mm, 1)

            def pT(j, bg, s):
                pe.wait_ge(weighed, UNITS * j + 2 * bg + 2)
                step = 3 * bg + s
                pe.wait_ge(pT_done, least(3 * BG * j + step - 1))
                for c in range(2 * s, min(2 * s + 2, NM)):
                    for t in range(2):
                        at = (c % 2) * N + t * P
                        last = pe.transpose(T[step % 2][:, at:at + P], flat[(2 * bg + t) % NP][:, c * P:(c + 1) * P], ident[:])
                last.then_inc(pT_mm, 1)

            def attend(j, bg):
                pe.wait_ge(vd_done, BG * j + bg + 1)
                pe.wait_ge(pT_done, 3 * (BG * j + bg) + 3)
                for c in range(NM):
                    last = pe.matmul(Q[:, 0:N], vd[:, bg, c], probsT[bg % 2][:, c], start=(c == 0), stop=(c == NM - 1))
                last.then_inc(o_mm, 1)

            def project(j, half):
                pe.wait_ge(setup_done, QKV_READY + 1)
                pe.wait_ge(o_lo_done, BG * j + 2 * half + 2)
                for t in (2 * half, 2 * half + 1):
                    tok = slice(t * P, (t + 1) * P)
                    last = product(Q[:, (t % 2) * C:(t % 2 + 1) * C],
                                   [((oT_hi[:, g, tok], oT_lo[:, g, tok]), (pw_hi[:, g], pw_lo[:, g])) for g in range(G)])
                last.then_inc(proj_mm, 1)

            def hT(j, k):
                pe.wait_ge(setup_done, ALL_READY)
                pe.wait_ge(hn_done, TT * (j + 1))
                pe.wait_ge(y_done, 2 * j)
                for t in range(TT):
                    last = pe.transpose(F[k][:, t * P:(t + 1) * P], hn[:, t, k * P:(k + 1) * P], ident[:])
                last.then_inc(hT_mm, 1)

            def fc1(j, k):
                pe.wait_ge(hT_lo_done, KC * (j + 1))
                if k >= 2:
                    pe.wait_ge(g_hi_done, least(HC * j + k - 1))
                cols = slice(k * P, (k + 1) * P)
                product(F[k % 2][:], [((w1_hi[:, c, cols], w1_lo[:, c, cols]), (hT_hi[:, c], hT_lo[:, c]))
                                      for c in range(KC)]).then_inc(f1_mm, 1)

            def fc2(j, t):
                pe.wait_ge(g_hi_done, HC * j + 7 + t // 2)
                pe.wait_ge(g_lo_done, HC * (j + 1))
                tok = slice(t * P, (t + 1) * P)
                last = product(F[t // 2][:, (t % 2) * C:(t % 2 + 1) * C],
                               [((g_hi[:, k, tok], g_lo[:, k, tok]), (w2_hi[:, k], w2_lo[:, k])) for k in range(HC)])
                if t % 2:
                    last.then_inc(f2_mm, 1)

            def bias_columns(raw, nb, at, cnt):
                for m in range(cnt):
                    for k in range(KC):
                        last = pe.matmul(F[0][:, at + m:at + m + 1], raw[:, k, m * P:(m + 1) * P], vecs[:, nb, k:k + 1],
                                         start=(k == 0), stop=(k == KC - 1))
                return last

            def fc1_bias():
                pe.wait_ge(mlp_loaded, 2 * 16)
                bias_columns(raw_w1, 5, 2 * G, HC).then_inc(bias_mm, 1)

            pe.wait_ge(consts, CONSTS)
            pe.wait_ge(vecs_loaded, 7 * 16)
            nv = 6 * KC + HC
            pe.transpose(F[1][:, 0:nv], vec_rows[:], ident[0:nv, 0:nv]).then_inc(vecs_mm, 1)
            cT(0)
            pe.wait_ge(vecs_done, 2)
            pe.wait_ge(qkv_loaded, 2 * 16)
            bias_columns(raw_q, 1, 0, G)
            bias_columns(raw_kv, 3, G, G).then_inc(bias_mm, 1)
            for k in range(KC):
                last = pe.matmul(F[1][0:M, 0:C], vecs[:, 3, k:k + 1].to_broadcast([P, M]), raw_kv[:, k, C:],
                                 start=(k == 0), stop=(k == KC - 1))
            last.then_inc(bias_mm, 1)

            pe.wait_ge(cT_lo_done, 1)
            xT(0, 0)
            pe.wait_ge(xT_lo_done, 1)
            pe.wait_ge(setup_done, QKV_READY)
            k_proj(0)
            pe.wait_ge(k_step, G)
            xT(0, 1)
            pe.wait_ge(xT_lo_done, 2)
            v_proj(0)
            pe.wait_ge(v_rows_done, 1)
            q_proj(0, 0)
            pe.wait_ge(q_lo_done, 2)
            q_proj(0, 1)
            pe.wait_ge(q_lo_done, 4)
            scores(0, 0, 0)
            scores(0, 0, 1)
            scores(0, 0, 2)
            scores(0, 0, 3)
            pT(0, 0, 0)
            pT(0, 0, 1)

            def body(j, par, mlp, prep, ahead):
                scores(j, par, 4)
                pT(j, 0, 2)
                pT(j, 1, 0)
                if mlp:
                    hT(j - 1, 0)
                    hT(j - 1, 1)
                pe.wait_ge(x1_done, 2 * j)
                attend(j, 0)
                pT(j, 1, 1)
                scores(j, par, 5)
                if mlp:
                    fc1(j - 1, 0)
                else:
                    fc1_bias()
                pT(j, 1, 2)
                if mlp:
                    fc1(j - 1, 1)
                scores(j, par, 6)
                if mlp:
                    fc1(j - 1, 2)
                if prep:
                    pe.wait_ge(xT_lo_done, KC * (j + 1))
                    cT(j + 1)
                pe.wait_ge(o_lo_done, BG * j + 1)
                attend(j, 1)
                if mlp:
                    fc1(j - 1, 3)
                if prep:
                    pe.wait_ge(cT_lo_done, j + 2)
                    k_proj(j + 1)
                pe.wait_ge(o_lo_done, BG * j + 2)
                project(j, 0)
                if prep:
                    pe.wait_ge(k_step, K_STEPS * (j + 1) + G)
                    xT(j + 1, 0)
                scores(j, par, 7)
                if prep:
                    pe.wait_ge(x1_done, 2 * j + 1)
                    v_proj(j + 1)
                    pe.wait_ge(xT_lo_done, KC * (j + 1) + 1)
                    xT(j + 1, 1)
                if mlp:
                    fc1(j - 1, 4)
                pT(j, 2, 0)
                if mlp:
                    fc1(j - 1, 5)
                if prep:
                    pe.wait_ge(v_rows_done, j + 2)
                    q_proj(j + 1, 0)
                pT(j, 2, 1)
                if mlp:
                    fc1(j - 1, 6)
                    fc1(j - 1, 7)
                pT(j, 2, 2)
                if prep:
                    pe.wait_ge(q_lo_done, 2 * (G * (j + 1) + 1))
                    q_proj(j + 1, 1)
                    scores(j + 1, 1 - par, 0)
                if mlp:
                    fc2(j - 1, 0)
                    fc2(j - 1, 1)
                pT(j, 3, 0)
                if prep:
                    scores(j + 1, 1 - par, 1)
                pT(j, 3, 1)
                if prep:
                    pe.wait_ge(q_lo_done, 2 * G * (j + 2))
                else:
                    pe.wait_ge(x1_done, 2 * j + 1)
                attend(j, 2)
                pT(j, 3, 2)
                if prep:
                    scores(j + 1, 1 - par, 2)
                pe.wait_ge(o_lo_done, BG * j + 3)
                attend(j, 3)
                if prep:
                    scores(j + 1, 1 - par, 3)
                if mlp:
                    fc2(j - 1, 2)
                pe.wait_ge(o_lo_done, BG * j + 4)
                project(j, 1)
                if prep:
                    pT(j + 1, 0, 0)
                if mlp:
                    fc2(j - 1, 3)
                if prep:
                    pT(j + 1, 0, 1)
            pairs_of(pe, body)
            last_pair = PAIRS - 1
            hT(last_pair, 0)
            hT(last_pair, 1)
            for k in range(HC):
                fc1(last_pair, k)
            for t in range(TT):
                fc2(last_pair, t)


CONSTS = 13
QKV_READY = 4 + 1 + 4 + 2
ALL_READY = QKV_READY + 1 + 8 + 1

_INS = ['x', 'ctx_1024', 'mask_BxSxS2_bk0', 'L0_xattn_qn_w', 'L0_xattn_qn_b', 'L0_xattn_cn_w', 'L0_xattn_cn_b',
        'L0_xattn_n2_w', 'L0_xattn_n2_b', 'L0_xattn_q_w', 'L0_xattn_kv_w', 'L0_xattn_proj_w', 'L0_xattn_proj_b',
        'L0_xattn_fc1_w', 'L0_xattn_fc1_b', 'L0_xattn_fc2_w', 'L0_xattn_fc2_b']


def kernel(**inputs):
    import numpy as _np
    import concourse.bacc as _bacc
    from concourse import mybir as _mybir
    from concourse.bass_utils import run_bass_kernel_spmd as _run

    nc = _bacc.Bacc("TRN2", target_bir_lowering=False, num_devices=1)
    arrays, args = {}, []
    for name in _INS:
        a = _np.ascontiguousarray(inputs[name])
        arrays[f"in_{name}"] = a
        args.append(nc.dram_tensor(f"in_{name}", a.shape, _mybir.dt.from_np(a.dtype), kind="ExternalInput").ap())
    shape = arrays["in_x"].shape
    args.append(nc.dram_tensor("out_0", shape, _mybir.dt.float32, kind="ExternalOutput").ap())
    xattn_block(nc, *args)
    r = _run(nc, [arrays], core_ids=[0])
    return r.results[0]["out_0"]
```
